# Optimizing a Trainium2 kernel written in Bass

```python
import numpy as np
import jax
import jax.numpy as jnp

def _softmax(x, axis=-1):
    return jax.nn.softmax(x, axis=axis)

def _gelu(x):
    return jax.nn.gelu(x, approximate=True)

def _silu(x):
    return jax.nn.silu(x)

def _sigmoid(x):
    return jax.nn.sigmoid(x)

def _layernorm(x, axis=-1, eps=1e-05):
    m = jnp.mean(x, axis=axis, keepdims=True)
    v = jnp.var(x, axis=axis, keepdims=True)
    return (x - m) / jnp.sqrt(v + eps)

def _scatter_add(tgt, idx, src, axis=0):
    return tgt.at[idx].add(src)

def _segment_sum(src, seg, n):
    return jax.ops.segment_sum(src, seg, n)
kernel_name = 'mk_hybrid_d1_jaxref_r4_520bee'

def setup_inputs(seed: int=0):
    np.random.seed(seed)
    _w = jnp.asarray

    def _L0_attn_a_setup():
        import jax, jax.numpy as jnp
        import numpy as np
        B, T = (4, 512)
        D_MODEL = 256
        N_HEADS = 8
        HEAD_DIM = 64
        KV_LRANK = 64

        def _orthogonalize_per_head(w):
            chunks = w.reshape(N_HEADS, HEAD_DIM, D_MODEL)

            def ns(m):
                A = m @ m.T
                Bm = 1.5 * jnp.eye(HEAD_DIM, dtype=m.dtype) - 0.5 * A
                return Bm @ m
            return jax.vmap(ns)(chunks).reshape(w.shape)
        key = jax.random.key(seed)
        ks = jax.random.split(key, 6)

        def lin(k, out_dim, in_dim):
            bound = 1.0 / np.sqrt(in_dim)
            return jax.random.uniform(k, (out_dim, in_dim), jnp.float32, -bound, bound)
        Wq = _orthogonalize_per_head(lin(ks[0], N_HEADS * HEAD_DIM, D_MODEL))
        return {'x': jax.random.normal(ks[1], (B, T, D_MODEL), jnp.float32), 'Wq': Wq, 'Wkv_down': lin(ks[2], KV_LRANK, D_MODEL), 'Wk_up': lin(ks[3], N_HEADS * HEAD_DIM, KV_LRANK), 'Wv_up': lin(ks[4], N_HEADS * HEAD_DIM, KV_LRANK), 'Wo': lin(ks[5], D_MODEL, N_HEADS * HEAD_DIM)}
    _L0_attn_a_in = _L0_attn_a_setup()

    def _L0_attn_b_setup():
        import jax, jax.numpy as jnp
        import numpy as np
        EMBED_DIM = 256
        NUM_HEADS = 16
        HEAD_DIM = EMBED_DIM // NUM_HEADS
        EPSILON = 1e-06
        SCORE_SCALE = 1.0
        B, L = (2, 512)
        key = jax.random.key(seed)
        k0, k1, k2, k3, k4 = jax.random.split(key, 5)
        s_in = 1.0 / np.sqrt(EMBED_DIM)
        return {'x': jax.random.normal(k0, (B, L, EMBED_DIM), dtype=jnp.float32), 'w_qkv': jax.random.normal(k1, (EMBED_DIM, 3 * EMBED_DIM), dtype=jnp.float32) * s_in, 'b_qkv': jnp.zeros((3 * EMBED_DIM,), dtype=jnp.float32), 'w_out': jax.random.normal(k2, (EMBED_DIM, EMBED_DIM), dtype=jnp.float32) * s_in, 'b_out': jnp.zeros((EMBED_DIM,), dtype=jnp.float32)}
    _L0_attn_b_in = _L0_attn_b_setup()

    def _L0_ffn_setup():
        import jax, jax.numpy as jnp
        import numpy as np
        DIM = 256
        DEPTH = 2
        HEADS = 8
        DIM_HEAD = 64
        WINDOW = 128
        INNER = HEADS * DIM_HEAD
        HID = int(DIM * 4 * 2 / 3)
        B, N = (2, 2048)
        QK_SCALE = 8.0

        def shift_token(t):
            t1, t2 = jnp.split(t, 2, axis=-1)
            t2 = jnp.pad(t2, ((0, 0), (1, 0), (0, 0)))[:, :-1]
            return jnp.concatenate([t1, t2], axis=-1)

        def l2norm(t):
            return t / jnp.clip(jnp.linalg.norm(t, axis=-1, keepdims=True), 1e-12)

        def rotate_half(x):
            x1, x2 = jnp.split(x, 2, axis=-1)
            return jnp.concatenate([-x2, x1], axis=-1)

        def rotary_xpos(q, k):
            n = q.shape[-2]
            half_idx = jnp.arange(0, DIM_HEAD, 2, dtype=jnp.float32)
            inv_freq = 1.0 / 10000.0 ** (half_idx / DIM_HEAD)
            t = jnp.arange(n, dtype=jnp.float32)
            freqs = t[:, None] * inv_freq[None, :]
            freqs = jnp.concatenate([freqs, freqs], axis=-1)
            base = (half_idx + 0.4 * DIM_HEAD) / (1.4 * DIM_HEAD)
            power = (t - n // 2) / float(WINDOW // 2)
            scale = base[None, :] ** power[:, None]
            scale = jnp.concatenate([scale, scale], axis=-1)
            cos, sin = (jnp.cos(freqs), jnp.sin(freqs))
            q = q * cos * scale + rotate_half(q) * sin * scale
            k = k * cos / scale + rotate_half(k) * sin / scale
            return (q, k)

        def local_attention(q, k, v):
            b, h, n, d = q.shape
            w = n // WINDOW
            bq = q.reshape(b, h, w, WINDOW, d) * QK_SCALE
            bk = k.reshape(b, h, w, WINDOW, d)
            bv = v.reshape(b, h, w, WINDOW, d)

            def look_around(t):
                p = jnp.pad(t, ((0, 0), (0, 0), (1, 0), (0, 0), (0, 0)))
                return jnp.concatenate([p[:, :, :w], p[:, :, 1:]], axis=3)
            bk, bv = (look_around(bk), look_around(bv))
            bt = jnp.arange(n).reshape(w, WINDOW)
            btp = jnp.pad(bt, ((1, 0), (0, 0)), constant_values=-1)
            btk = jnp.concatenate([btp[:w], btp[1:]], axis=1)
            sim = jnp.einsum('bhwid,bhwjd->bhwij', bq, bk)
            i = bt[:, :, None]
            j = btk[:, None, :]
            mask = (i < j) | (i > j + WINDOW) | (j == -1)
            sim = jnp.where(mask, -jnp.finfo(sim.dtype).max, sim)
            attn = jax.nn.softmax(sim, axis=-1)
            out = jnp.einsum('bhwij,bhwjd->bhwid', attn, bv)
            return out.reshape(b, h, n, d)

        def _layer(x, wqkv, qs, ksc, wo, lg, lb, w1, b1, w2, b2):
            b, n, _ = x.shape
            h = shift_token(x)
            qkv = h @ wqkv
            q, k, v = jnp.split(qkv, 3, axis=-1)
            to_heads = lambda t: t.reshape(b, n, HEADS, DIM_HEAD).transpose(0, 2, 1, 3)
            q, k, v = (to_heads(q), to_heads(k), to_heads(v))
            q = l2norm(q) * qs
            k = l2norm(k) * ksc
            q, k = rotary_xpos(q, k)
            o = local_attention(q, k, v)
            o = o.transpose(0, 2, 1, 3).reshape(b, n, INNER)
            x = x + o @ wo
            h = shift_token(x)
            mu = h.mean(-1, keepdims=True)
            var = h.var(-1, keepdims=True)
            h = (h - mu) / jnp.sqrt(var + 1e-05) * lg + lb
            h = h @ w1 + b1
            a, g = jnp.split(h, 2, axis=-1)
            h = a * jax.nn.gelu(g, approximate=False)
            x = x + h @ w2 + b2
            return x
        key = jax.random.key(seed)
        ks = jax.random.split(key, 6)
        return {'x': jax.random.normal(ks[0], (B, N, DIM), jnp.float32), 'wqkv': jax.random.normal(ks[1], (DEPTH, DIM, 3 * INNER), jnp.float32) * 0.02, 'q_scale': jnp.ones((DEPTH, DIM_HEAD), jnp.float32), 'k_scale': jnp.ones((DEPTH, DIM_HEAD), jnp.float32), 'wo': jax.random.normal(ks[2], (DEPTH, INNER, DIM), jnp.float32) * 0.02, 'ln_g': jnp.ones((DEPTH, DIM), jnp.float32), 'ln_b': jnp.zeros((DEPTH, DIM), jnp.float32), 'w1': jax.random.normal(ks[3], (DEPTH, DIM, 2 * HID), jnp.float32) * 0.02, 'b1': jnp.zeros((DEPTH, 2 * HID), jnp.float32), 'w2': jax.random.normal(ks[4], (DEPTH, HID, DIM), jnp.float32) * 0.02, 'b2': jnp.zeros((DEPTH, DIM), jnp.float32)}
    _L0_ffn_in = _L0_ffn_setup()
    _d = {'L0_attn_a_x': _L0_attn_a_in['x'], 'L0_attn_a_Wq': _L0_attn_a_in['Wq'], 'L0_attn_a_Wkv_down': _L0_attn_a_in['Wkv_down'], 'L0_attn_a_Wk_up': _L0_attn_a_in['Wk_up'], 'L0_attn_a_Wv_up': _L0_attn_a_in['Wv_up'], 'L0_attn_a_Wo': _L0_attn_a_in['Wo'], 'L0_attn_b_w_qkv': _L0_attn_b_in['w_qkv'], 'L0_attn_b_b_qkv': _L0_attn_b_in['b_qkv'], 'L0_attn_b_w_out': _L0_attn_b_in['w_out'], 'L0_attn_b_b_out': _L0_attn_b_in['b_out'], 'L0_ffn_wqkv': _L0_ffn_in['wqkv'], 'L0_ffn_q_scale': _L0_ffn_in['q_scale'], 'L0_ffn_k_scale': _L0_ffn_in['k_scale'], 'L0_ffn_wo': _L0_ffn_in['wo'], 'L0_ffn_ln_g': _L0_ffn_in['ln_g'], 'L0_ffn_ln_b': _L0_ffn_in['ln_b'], 'L0_ffn_w1': _L0_ffn_in['w1'], 'L0_ffn_b1': _L0_ffn_in['b1'], 'L0_ffn_w2': _L0_ffn_in['w2'], 'L0_ffn_b2': _L0_ffn_in['b2']}
    _x0 = _d['L0_attn_a_x']
    _d['L0_attn_a_x'] = jax.random.normal(jax.random.fold_in(jax.random.key(seed), 1), (8, 512, 256), dtype=_x0.dtype)
    del _x0
    return _d

def reference(L0_attn_a_x, L0_attn_a_Wq, L0_attn_a_Wkv_down, L0_attn_a_Wk_up, L0_attn_a_Wv_up, L0_attn_a_Wo, L0_attn_b_w_qkv, L0_attn_b_b_qkv, L0_attn_b_w_out, L0_attn_b_b_out, L0_ffn_wqkv, L0_ffn_q_scale, L0_ffn_k_scale, L0_ffn_wo, L0_ffn_ln_g, L0_ffn_ln_b, L0_ffn_w1, L0_ffn_b1, L0_ffn_w2, L0_ffn_b2):

    def _L0_attn_a_ref(x, Wq, Wkv_down, Wk_up, Wv_up, Wo):
        import jax, jax.numpy as jnp
        import numpy as np
        B, T = (4, 512)
        D_MODEL = 256
        N_HEADS = 8
        HEAD_DIM = 64
        KV_LRANK = 64

        def _orthogonalize_per_head(w):
            chunks = w.reshape(N_HEADS, HEAD_DIM, D_MODEL)

            def ns(m):
                A = m @ m.T
                Bm = 1.5 * jnp.eye(HEAD_DIM, dtype=m.dtype) - 0.5 * A
                return Bm @ m
            return jax.vmap(ns)(chunks).reshape(w.shape)
        b, t, _ = x.shape
        q = (x @ Wq.T).reshape(b, t, N_HEADS, HEAD_DIM)
        kv_latent = x @ Wkv_down.T
        k = (kv_latent @ Wk_up.T).reshape(b, t, N_HEADS, HEAD_DIM)
        v = (kv_latent @ Wv_up.T).reshape(b, t, N_HEADS, HEAD_DIM)
        scale = HEAD_DIM ** (-0.5)
        scores = jnp.einsum('bqhd,bkhd->bhqk', q, k) * scale
        attn = jax.nn.softmax(scores, axis=-1)
        out = jnp.einsum('bhqk,bkhd->bqhd', attn, v)
        out = out.reshape(b, t, N_HEADS * HEAD_DIM)
        return out @ Wo.T

    def _L0_attn_b_ref(x, w_qkv, b_qkv, w_out, b_out):
        import jax, jax.numpy as jnp
        import numpy as np
        EMBED_DIM = 256
        NUM_HEADS = 16
        HEAD_DIM = EMBED_DIM // NUM_HEADS
        EPSILON = 1e-06
        SCORE_SCALE = 1.0
        B, L = (2, 512)
        Bq, Lq, E = x.shape
        qkv = x @ w_qkv + b_qkv
        q, k, v = jnp.split(qkv, 3, axis=-1)
        q = q.reshape(Bq, Lq, NUM_HEADS, HEAD_DIM).transpose(0, 2, 1, 3)
        k = k.reshape(Bq, Lq, NUM_HEADS, HEAD_DIM).transpose(0, 2, 1, 3)
        v = v.reshape(Bq, Lq, NUM_HEADS, HEAD_DIM).transpose(0, 2, 1, 3)
        dot = jnp.einsum('bhid,bhjd->bhij', q, k)
        q_norm_sq = jnp.sum(q * q, axis=-1, keepdims=True)
        k_norm_sq = jnp.sum(k * k, axis=-1, keepdims=True)
        vals = q_norm_sq + k_norm_sq.transpose(0, 1, 3, 2)
        scores = dot * dot / (vals - 2.0 * dot + EPSILON) * SCORE_SCALE
        mask = jnp.triu(jnp.ones((Lq, Lq), dtype=scores.dtype), k=1) * -1000000000.0
        scores = scores + mask[None, None, :, :]
        attn = jax.nn.softmax(scores, axis=-1)
        out = jnp.einsum('bhij,bhjd->bhid', attn, v)
        out = out.transpose(0, 2, 1, 3).reshape(Bq, Lq, E)
        return out @ w_out + b_out

    def _L0_ffn_ref(x, wqkv, q_scale, k_scale, wo, ln_g, ln_b, w1, b1, w2, b2):
        import jax, jax.numpy as jnp
        import numpy as np
        DIM = 256
        DEPTH = 2
        HEADS = 8
        DIM_HEAD = 64
        WINDOW = 128
        INNER = HEADS * DIM_HEAD
        HID = int(DIM * 4 * 2 / 3)
        B, N = (2, 2048)
        QK_SCALE = 8.0

        def shift_token(t):
            t1, t2 = jnp.split(t, 2, axis=-1)
            t2 = jnp.pad(t2, ((0, 0), (1, 0), (0, 0)))[:, :-1]
            return jnp.concatenate([t1, t2], axis=-1)

        def l2norm(t):
            return t / jnp.clip(jnp.linalg.norm(t, axis=-1, keepdims=True), 1e-12)

        def rotate_half(x):
            x1, x2 = jnp.split(x, 2, axis=-1)
            return jnp.concatenate([-x2, x1], axis=-1)

        def rotary_xpos(q, k):
            n = q.shape[-2]
            half_idx = jnp.arange(0, DIM_HEAD, 2, dtype=jnp.float32)
            inv_freq = 1.0 / 10000.0 ** (half_idx / DIM_HEAD)
            t = jnp.arange(n, dtype=jnp.float32)
            freqs = t[:, None] * inv_freq[None, :]
            freqs = jnp.concatenate([freqs, freqs], axis=-1)
            base = (half_idx + 0.4 * DIM_HEAD) / (1.4 * DIM_HEAD)
            power = (t - n // 2) / float(WINDOW // 2)
            scale = base[None, :] ** power[:, None]
            scale = jnp.concatenate([scale, scale], axis=-1)
            cos, sin = (jnp.cos(freqs), jnp.sin(freqs))
            q = q * cos * scale + rotate_half(q) * sin * scale
            k = k * cos / scale + rotate_half(k) * sin / scale
            return (q, k)

        def local_attention(q, k, v):
            b, h, n, d = q.shape
            w = n // WINDOW
            bq = q.reshape(b, h, w, WINDOW, d) * QK_SCALE
            bk = k.reshape(b, h, w, WINDOW, d)
            bv = v.reshape(b, h, w, WINDOW, d)

            def look_around(t):
                p = jnp.pad(t, ((0, 0), (0, 0), (1, 0), (0, 0), (0, 0)))
                return jnp.concatenate([p[:, :, :w], p[:, :, 1:]], axis=3)
            bk, bv = (look_around(bk), look_around(bv))
            bt = jnp.arange(n).reshape(w, WINDOW)
            btp = jnp.pad(bt, ((1, 0), (0, 0)), constant_values=-1)
            btk = jnp.concatenate([btp[:w], btp[1:]], axis=1)
            sim = jnp.einsum('bhwid,bhwjd->bhwij', bq, bk)
            i = bt[:, :, None]
            j = btk[:, None, :]
            mask = (i < j) | (i > j + WINDOW) | (j == -1)
            sim = jnp.where(mask, -jnp.finfo(sim.dtype).max, sim)
            attn = jax.nn.softmax(sim, axis=-1)
            out = jnp.einsum('bhwij,bhwjd->bhwid', attn, bv)
            return out.reshape(b, h, n, d)

        def _layer(x, wqkv, qs, ksc, wo, lg, lb, w1, b1, w2, b2):
            b, n, _ = x.shape
            h = shift_token(x)
            qkv = h @ wqkv
            q, k, v = jnp.split(qkv, 3, axis=-1)
            to_heads = lambda t: t.reshape(b, n, HEADS, DIM_HEAD).transpose(0, 2, 1, 3)
            q, k, v = (to_heads(q), to_heads(k), to_heads(v))
            q = l2norm(q) * qs
            k = l2norm(k) * ksc
            q, k = rotary_xpos(q, k)
            o = local_attention(q, k, v)
            o = o.transpose(0, 2, 1, 3).reshape(b, n, INNER)
            x = x + o @ wo
            h = shift_token(x)
            mu = h.mean(-1, keepdims=True)
            var = h.var(-1, keepdims=True)
            h = (h - mu) / jnp.sqrt(var + 1e-05) * lg + lb
            h = h @ w1 + b1
            a, g = jnp.split(h, 2, axis=-1)
            h = a * jax.nn.gelu(g, approximate=False)
            x = x + h @ w2 + b2
            return x
        for l in range(DEPTH):
            x = _layer(x, wqkv[l], q_scale[l], k_scale[l], wo[l], ln_g[l], ln_b[l], w1[l], b1[l], w2[l], b2[l])
        return x
    x = L0_attn_a_x
    x = x + _L0_attn_a_ref(_layernorm(x, axis=-1), L0_attn_a_Wq, L0_attn_a_Wkv_down, L0_attn_a_Wk_up, L0_attn_a_Wv_up, L0_attn_a_Wo)
    x = x + _L0_ffn_ref(_layernorm(x, axis=-1), L0_ffn_wqkv, L0_ffn_q_scale, L0_ffn_k_scale, L0_ffn_wo, L0_ffn_ln_g, L0_ffn_ln_b, L0_ffn_w1, L0_ffn_b1, L0_ffn_w2, L0_ffn_b2)
    x = x + _L0_attn_b_ref(_layernorm(x, axis=-1), L0_attn_b_w_qkv, L0_attn_b_b_qkv, L0_attn_b_w_out, L0_attn_b_b_out)
    x = x + _L0_ffn_ref(_layernorm(x, axis=-1), L0_ffn_wqkv, L0_ffn_q_scale, L0_ffn_k_scale, L0_ffn_wo, L0_ffn_ln_g, L0_ffn_ln_b, L0_ffn_w1, L0_ffn_b1, L0_ffn_w2, L0_ffn_b2)
    return x

_drawn_inputs = setup_inputs


def setup_inputs(seed=0):
    import zlib

    import numpy as np

    out = dict(_drawn_inputs(seed))
    spreads = {'L0_attn_b_b_qkv': (0.0, 0.328),
     'L0_attn_b_b_out': (0.0, 0.782),
     'L0_ffn_q_scale': (1.0, 0.6),
     'L0_ffn_k_scale': (1.0, 0.6),
     'L0_ffn_ln_g': (1.0, 0.6),
     'L0_ffn_ln_b': (0.0, 2.0),
     'L0_ffn_b1': (0.0, 1.106),
     'L0_ffn_b2': (0.0, 0.313)}
    factors = {'L0_attn_a_Wq': 4.74,
     'L0_attn_a_Wkv_down': 4.104,
     'L0_attn_a_Wk_up': 4.708,
     'L0_attn_a_Wv_up': 3.374,
     'L0_attn_a_Wo': 3.312,
     'L0_ffn_wqkv': 4.325,
     'L0_ffn_wo': 4.295}
    for name, (base, spread) in spreads.items():
        noise = np.random.default_rng([zlib.crc32(name.encode()), seed]).standard_normal(out[name].shape)
        drawn = base * np.exp(spread * noise) if base else spread * noise
        out[name] = jnp.asarray(drawn.astype(out[name].dtype))
    for name, factor in factors.items():
        out[name] = (out[name] * factor).astype(out[name].dtype)
    return out
```

```python
from contextlib import ExitStack

import numpy as np

import concourse.bass as bass
from concourse import mybir

F32 = mybir.dt.float32
ALU = mybir.AluOpType
ACT = mybir.ActivationFunctionType
AX = mybir.AxisListType.X

P = 128
SEQS, TOKENS, DIM = 8, 512, 256
TILES = TOKENS // P
FC = DIM // P
HEADS, HD = 8, 64
INNER = HEADS * HD
PAIRS = HEADS // 2
RANK = 64
BHEADS, BHD, BROW = 16, 16, 32
GROUPS = BHEADS * BROW // P
HID = int(DIM * 4 * 2 / 3)
HC = -(-HID // P)
HLAST = HID - (HC - 1) * P
DEPTH = 2
EPS_LN, EPS_B = 1e-5, 1e-6
MASKED = -1e30
LOW = 3e38


class Mark:

    def __init__(self, sem, value):
        self.sem, self.value = sem, value


class Signals:

    def __init__(self, nc, stack):
        self.nc, self.stack, self.sems, self.counts = nc, stack, {}, {}

    def restart(self):
        self.counts = {}

    def count(self, name, step):
        if name not in self.sems:
            self.sems[name] = self.stack.enter_context(self.nc.semaphore("s_" + name))
        self.counts[name] = self.counts.get(name, 0) + step
        return Mark(self.sems[name], self.counts[name])


class Queue:

    def __init__(self, name, signals, eng):
        self.name, self.signals, self.eng, self.seen = name, signals, eng, {}

    def do(self, emit, waits=(), signal="done", step=1):
        mark = self.signals.count(f"{self.name}_{signal}", step)
        if self.eng is not None:
            self.wait(waits)
            emit(self.eng).then_inc(mark.sem, step)
        return mark

    def wait(self, waits):
        if self.eng is None:
            return
        for mark in flat(waits):
            if self.seen.get(id(mark.sem), 0) < mark.value:
                self.seen[id(mark.sem)] = mark.value
                self.eng.wait_ge(mark.sem, mark.value)


def flat(waits):
    if isinstance(waits, Mark):
        return [waits]
    return [m for w in waits for m in flat(w)]


class Slot:

    def __init__(self, buf):
        self.buf, self.free, self.taken = buf, [], False


class Ring:

    def __init__(self, bufs):
        self.slots, self.next = [Slot(b) for b in bufs], 0

    def take(self):
        slot = self.slots[self.next % len(self.slots)]
        assert not slot.taken, "a ring's buffer is still in use"
        slot.taken = True
        self.next += 1
        return slot

    @staticmethod
    def give(slot, *marks):
        slot.free, slot.taken = list(marks), False


def build(nc, d):
    stack = ExitStack()
    with stack:
        sig = Signals(nc, stack)
        def sb(name, *shape):
            return stack.enter_context(nc.sbuf_tensor(name, [P, *shape], F32))

        resid = sb("resid", SEQS, TILES, DIM)
        w_in = sb("w_in", 3072)
        w_out = sb("w_out", 1024)
        w_up = sb("w_up", FC, 2 * HID)
        w_down = sb("w_down", HC, DIM)
        rot = sb("rot", 4, TILES, HD)
        qk_scale = sb("qk_scale", 2, HD)
        ln_gb = sb("ln_gb", 2, FC)
        bias_up = sb("bias_up", 2 * HC)
        bias_row = sb("bias_row", DIM)
        ident = sb("ident", P)
        local_mask = sb("local_mask", 2 * P)
        causal_mask = sb("causal_mask", TOKENS)
        minus_half = sb("minus_half", 64)
        dot_rows = sb("dot_rows", 1)
        work = [sb(f"work{s}", 3, 4 * TOKENS) for s in range(2)]
        kpad = [sb(f"kpad{s}", 8 * TOKENS) for s in range(2)]
        x_t = [sb(f"x_t{s}", FC, TOKENS + 1) for s in range(2)]
        x_n = [sb(f"x_n{s}", TILES, DIM) for s in range(2)]
        shifted = [sb(f"shifted{s}", TILES, P) for s in range(2)]
        stat = [sb(f"stat{s}", 256) for s in range(2)]
        rows = sb("rows", 2, 2 * TOKENS)
        scratch_buf = sb("scratch", 2 * TOKENS)
        prob_own = [sb(f"prob{s}", 2 * TOKENS) for s in range(2)]
        prob_t_bufs = [sb(f"prob_t{i}", 2 * TOKENS) for i in range(2)]
        small_bufs = [sb(f"small{i}", 16) for i in range(16)]

        wide_bufs = [stack.enter_context(nc.psum_tensor(f"wide{i}", [P, 1024], F32)) for i in range(3)]
        narrow_bufs = [stack.enter_context(nc.psum_tensor(f"narrow{i}", [P, 512], F32)) for i in range(2)]

        def schedule(live, eng):
            sig.restart()
            pe, act, dve, pool, sp = (Queue(n, sig, eng if n2 == live else None) for n, n2 in (
                ("pe", "tensor"), ("act", "scalar"), ("dve", "vector"), ("pool", "gpsimd"), ("sp", "sync")))
            small = Ring(small_bufs)
            scratch = Ring([scratch_buf])
            prob_t = Ring(prob_t_bufs)
            wide = Ring(wide_bufs)
            narrow = [Ring([buf]) for buf in narrow_bufs]
            def load(dst, src, waits, signal):
                return sp.do(lambda e: e.dma_start(dst, src, allow_slow_non_contiguous=True), waits, signal, 16)

            consts = [
                load(ident[:, :], d["ident"], [], "const"),
                load(local_mask[:, :], d["local_mask"], [], "const"),
                load(causal_mask[:, :], d["causal_mask"], [], "const"),
                load(dot_rows[:, :], d["dot_rows"], [], "const"),
            ][-1]
            consts = [consts, pool.do(lambda e: e.memset(minus_half[:, :], -0.5), [], "zero")]
            arrived = [load(resid[:, b], d["x"][b].rearrange("(t p) f -> p t f", p=P), [], f"x{b}")
                       for b in range(SEQS)]
            resid_done = [[m] for m in arrived]
            for s in range(2):
                first = pool.do(lambda e, s=s: e.memset(x_t[s][:, :, 0:1], 0.0), [], "zero")
                first = pool.do(lambda e, s=s: e.memset(shifted[s][:, :, :], 0.0), [], "zero")
                consts.append(first)

            weights = {}
            weight_users = {k: [] for k in ("w_in", "w_out", "w_up", "w_down", "small")}
            stream_free = [[], []]

            def mm(out, lhsT, rhs, start, stop, **k):
                return lambda e: e.matmul(out, lhsT, rhs, start=start, stop=stop, skip_group_check=True, **k)

            def tr(out, in_):
                return lambda e: e.transpose(out, in_, ident[0:in_.shape[0], 0:in_.shape[0]])

            def norm_stats(s, pieces, waits):
                st = stat[s]
                n = len(pieces(0))
                for t in range(TILES):
                    for i, piece in enumerate(pieces(t)):
                        got = dve.do(lambda e, t=t, i=i, piece=piece: e.bn_stats(
                            st[:, (t * 2 + i) * 6:(t * 2 + i) * 6 + 6], piece), waits, "stat")
                for t in range(TILES):
                    got = dve.do(lambda e, t=t: e.bn_aggr(
                        st[:, 64 + 2 * t:66 + 2 * t], st[:, t * 12:t * 12 + 6 * n]), got, "stat")
                var = st[:, 64:64 + 2 * TILES].rearrange("p (t c) -> p t c", c=2)[:, :, 1]
                eps = dve.do(lambda e: e.tensor_scalar(st[:, 80:80 + TILES], var, EPS_LN, None, ALU.add), got, "stat")
                power = pool.do(lambda e: e.tensor_tensor(st[:, 96:96 + TILES], st[:, 80:80 + TILES],
                                                          minus_half[:, 0:TILES], ALU.pow), [eps, consts], "rstd")
                return [got, power]

            def normalised(s, t, dst, src, waits):
                st = stat[s]
                return dve.do(lambda e: e.tensor_scalar(dst, src, st[:, 64 + 2 * t:65 + 2 * t],
                                                        st[:, 96 + t:97 + t], ALU.subtract, ALU.mult), waits, "norm")

            def to_features(s, src, waits, shift, scaled=None):
                done = []
                tile = wide.take()
                for c in range(FC):
                    for t in range(TILES):
                        last = pe.do(tr(tile.buf[:, c * TOKENS + t * P:c * TOKENS + (t + 1) * P],
                                        src(t)[:, c * P:(c + 1) * P]), [waits, tile.free, consts], "turn")
                for c in range(FC):
                    dst = x_t[s][:, c, 1:1 + TOKENS]
                    ps = tile.buf[:, c * TOKENS:(c + 1) * TOKENS]
                    if scaled is None:
                        done.append(act.do(lambda e, dst=dst, ps=ps: e.activation(dst, ps, ACT.Copy),
                                           [last, stream_free[s]], "x_t"))
                    else:
                        done.append(dve.do(lambda e, dst=dst, ps=ps, c=c: e.tensor_scalar(
                            dst, ps, ln_gb[:, 0, c:c + 1], ln_gb[:, 1, c:c + 1], ALU.mult, ALU.add),
                            [last, stream_free[s], scaled], "x_t"))
                wide.give(tile, done)
                return done

            def project_out(s, b, out_t, chunks, rows_done, extra=None):
                tile = wide.take()
                for t in range(TILES):
                    for c in range(chunks):
                        last = pe.do(mm(tile.buf[:, t * DIM:(t + 1) * DIM], out_t(c)[:, t * P:(t + 1) * P],
                                        w_out[:, c * DIM:(c + 1) * DIM], c == 0, c == chunks - 1),
                                     [rows_done, tile.free, weights["w_out"]], "proj")
                dst = resid[:, b].rearrange("p t f -> p (t f)")
                added = dve.do(lambda e: e.tensor_tensor(dst, tile.buf[:, :], dst, ALU.add), [last, resid_done[b]], "resid")
                wide.give(tile, added)
                weight_users["w_out"] = [last]
                return last, added

            def local_layer(s, b, depth, is_first, is_last):
                q_t = work[s][:, 0].rearrange("p (c n) -> p c n", c=PAIRS)
                v = work[s][:, 1].rearrange("p (t n) -> p t n", t=TILES)
                o_t = work[s][:, 2].rearrange("p (c n) -> p c n", c=PAIRS)
                k_p = kpad[s][:, :].rearrange("p (c j n) -> p c j n", c=PAIRS, j=2)
                flat_resid = resid[:, b].rearrange("p t f -> p (t f)")
                if is_first:
                    saved = sp.do(lambda e: e.dma_start(d["saved"][b], flat_resid), resid_done[b], f"saved{b}", 16)
                    stats = norm_stats(s, lambda t: [resid[:, b, t, :]], [resid_done[b], stream_free[s]])
                    yield
                    for t in range(TILES):
                        done = normalised(s, t, resid[:, b, t, :], resid[:, b, t, :], [stats, saved])
                    resid_done[b] = [done]
                    saves[b] = saved
                    yield
                ready = to_features(s, lambda t: resid[:, b, t, :], [resid_done[b]], True)
                yield
                ends = []
                for t in range(TILES):
                    raw, part2 = rows[:, 0, :], rows[:, 1, :]
                    part = x_n[s][:, :, :].rearrange("p t f -> p (t f)")
                    tile, vtile = wide.take(), wide.take()
                    for third, dst in ((0, tile.buf[:, 0:512]), (1, tile.buf[:, 512:1024]), (2, vtile.buf[:, 0:512])):
                        for c in range(FC):
                            last = pe.do(mm(dst, x_t[s][:, c, 1 - c + t * P:1 - c + (t + 1) * P],
                                            w_in[:, c * 3 * INNER + third * INNER:c * 3 * INNER + (third + 1) * INNER],
                                            c == 0, c == FC - 1),
                                         [ready, weights["w_in"], tile.free, vtile.free], "qkv")
                    got_v = act.do(lambda e, t=t: e.activation(v[:, t, :], vtile.buf[:, 0:512], ACT.Copy),
                                   [last, stream_free[s]], "v")
                    wide.give(vtile, got_v)
                    heads = lambda a: a.rearrange("p (h e) -> p h e", e=HD)
                    sq = scratch.take()
                    squared = act.do(lambda e: e.activation(sq.buf[:, :], tile.buf[:, :], ACT.Square),
                                     [last, sq.free], "square")
                    copied = act.do(lambda e: e.activation(raw, tile.buf[:, :], ACT.Copy),
                                    [last, rows_free["raw"]], "raw")
                    for z in range(2):
                        cosd = dve.do(lambda e, z=z, t=t: e.tensor_tensor(
                            heads(part[:, z * INNER:(z + 1) * INNER]), heads(tile.buf[:, z * INNER:(z + 1) * INNER]),
                            rot[:, 2 * z, t, :].unsqueeze(1).to_broadcast([P, HEADS, HD]), ALU.mult),
                            [copied, xn_free[s], weights["small"]], "cos")
                        halves = lambda a: a.rearrange("p (h u e) -> p h u e", u=2, e=HD // 2)
                        sind = pool.do(lambda e, z=z, t=t: e.tensor_tensor(
                            halves(part2[:, z * INNER:(z + 1) * INNER]),
                            halves(raw[:, z * INNER:(z + 1) * INNER])[:, :, ::-1, :],
                            rot[:, 2 * z + 1, t, :].rearrange("p (u e) -> p u e", u=2).unsqueeze(1)
                            .to_broadcast([P, HEADS, 2, HD // 2]), ALU.mult),
                            [copied, rows_free["sin"], weights["small"]], "sin")
                    wide.give(tile, squared, copied, cosd)
                    rows_free["raw"] = [sind]
                    ss = small.take()
                    summed = dve.do(lambda e: e.tensor_reduce(ss.buf[:, 0:16], sq.buf[:, :].rearrange(
                        "p (h e) -> p h e", e=HD), AX, ALU.add), [squared, ss.free], "ss")
                    scratch.give(sq, summed)
                    clipped = dve.do(lambda e: e.tensor_scalar(ss.buf[:, 0:16], ss.buf[:, 0:16], 1e-24, None, ALU.max),
                                     summed, "ss")
                    rn = small.take()
                    power = pool.do(lambda e: e.tensor_tensor(rn.buf[:, 0:16], ss.buf[:, 0:16], minus_half[:, 0:16],
                                                              ALU.pow), [clipped, rn.free, consts], "rn")
                    small.give(ss, power)
                    turned = pool.do(lambda e: e.tensor_tensor(part2, part, part2, ALU.add), [cosd, sind], "turned")
                    scaled = pool.do(lambda e: e.tensor_tensor(
                        heads(part), heads(part2), rn.buf[:, 0:16].unsqueeze(2).to_broadcast([P, 16, HD]), ALU.mult),
                        [turned, power], "scaled")
                    small.give(rn, scaled)
                    rows_free["sin"] = [scaled]
                    yield
                    tile = wide.take()
                    for z in range(8):
                        last = pe.do(tr(tile.buf[:, z * P:(z + 1) * P], part[:, z * P:(z + 1) * P]),
                                     [scaled, tile.free], "turn")
                    xn_free[s] = [last]
                    packed = tile.buf[:, :].rearrange("p (z c n) -> p z c n", z=2, c=PAIRS)
                    got_q = act.do(lambda e, t=t: e.activation(q_t[:, :, t * P:(t + 1) * P], packed[:, 0], ACT.Copy),
                                   [last, stream_free[s]], "q_t")
                    for j in range(2):
                        r = slice(64 * j, 64 * j + 64)
                        got_k = dve.do(lambda e, t=t, j=j, r=r: e.tensor_copy(k_p[r, :, j, t * P:(t + 1) * P], packed[r, 1]),
                                       [last, stream_free[s], kpad_zero[s]], "k_t")
                    wide.give(tile, got_q, got_k)
                    ends += [got_q, got_k, got_v]
                    yield
                weight_users["w_in"] = [ends[-1]]
                ready = ends
                out_marks = []
                for h in range(HEADS):
                    c, j = h // 2, h % 2
                    if j == 0:
                        o_tile = narrow[s].take()
                    tile = wide.take()
                    for t in range(TILES):
                        k0 = P * max(t - 1, 0)
                        dst = tile.buf[:, 256 * t + (P if t == 0 else 0):256 * (t + 1)]
                        last = pe.do(mm(dst, q_t[:, c, t * P:(t + 1) * P], k_p[:, c, j, k0:(t + 1) * P], True, True),
                                     [ready, tile.free], "score")
                    st = small.take()
                    pr = probs[s].take()
                    for t in range(TILES):
                        lo = 256 * t + (P if t == 0 else 0)
                        cut = slice(lo, 256 * (t + 1))
                        low = dve.do(lambda e, t=t, cut=cut, lo=lo: e.tensor_tensor_reduce(
                            pr.buf[:, cut], tile.buf[:, cut], local_mask[:, lo - 256 * t:256],
                            -1.0, LOW, ALU.add, ALU.min, st.buf[:, t:t + 1]),
                            [last, pr.free, st.free, consts], "max")
                        done = act.do(lambda e, t=t, cut=cut: e.activation(
                            pr.buf[:, cut], pr.buf[:, cut], ACT.Exp, bias=st.buf[:, t:t + 1], scale=-1.0,
                            accum_out=st.buf[:, 4 + t:5 + t]), [low], "exp")
                    wide.give(tile, low)
                    inv = dve.do(lambda e: e.reciprocal(st.buf[:, 8:12], st.buf[:, 4:8]), done, "inv")
                    for t in range(TILES):
                        lo = 256 * t + (P if t == 0 else 0)
                        cut = slice(lo, 256 * (t + 1))
                        scaled = pool.do(lambda e, t=t, cut=cut: e.tensor_scalar(
                            pr.buf[:, cut], pr.buf[:, cut], st.buf[:, 8 + t:9 + t], 1.0, ALU.mult, ALU.mult),
                            [inv, done], "weight")
                    small.give(st, scaled)
                    yield
                    tile, pt = wide.take(), prob_t.take()
                    for kb in range(TILES):
                        for t in range(kb, min(kb + 2, TILES)):
                            col = 256 * t + (P if t == kb else 0)
                            last = pe.do(tr(tile.buf[:, 256 * kb + P * (t - kb):256 * kb + P * (t - kb + 1)],
                                            pr.buf[:, col:col + P]), [scaled, tile.free], "turn")
                    Ring.give(pr, last)
                    got1 = act.do(lambda e: e.activation(pt.buf[:, 0:512], tile.buf[:, 0:512], ACT.Copy),
                                  [last, pt.free], "prob_t")
                    got2 = dve.do(lambda e: e.tensor_copy(pt.buf[:, 512:896], tile.buf[:, 512:896]),
                                  [last, pt.free], "prob_t")
                    wide.give(tile, got1, got2)
                    for kb in range(TILES):
                        n = P * min(2, TILES - kb)
                        last = pe.do(mm(o_tile.buf[64 * j:64 * j + 64, P * kb:P * kb + n],
                                        v[:, kb, h * HD:(h + 1) * HD], pt.buf[:, 256 * kb:256 * kb + n],
                                        kb == 0, kb == TILES - 1), [got1, got2, o_tile.free if j == 0 else []], "mix")
                    prob_t.give(pt, last)
                    if j == 1:
                        done = act.do(lambda e, c=c, o=o_tile: e.activation(o_t[:, c, :], o.buf[:, :], ACT.Copy),
                                      [last, stream_free[s]], "o_t")
                        Ring.give(o_tile, done)
                        out_marks.append(done)
                    yield
                o_read, added = project_out(s, b, lambda c: o_t[:, c, :], PAIRS, out_marks)
                resid_done[b] = [added]
                yield
                moved = [
                    sp.do(lambda e: e.dma_start(shifted[s][1:P, :, :], resid[0:P - 1, b, :, P:DIM]),
                          [added, shift_free[s]], f"shift{s}", 16),
                    sp.do(lambda e: e.dma_start(shifted[s][0:1, 1:TILES, :], resid[P - 1:P, b, 0:TILES - 1, P:DIM]),
                          [added, shift_free[s]], f"shift{s}", 16)]
                stats = norm_stats(s, lambda t: [resid[:, b, t, 0:P], shifted[s][:, t, :]], [added, moved[-1], consts])
                yield
                for t in range(TILES):
                    normalised(s, t, x_n[s][:, t, 0:P], resid[:, b, t, 0:P], [stats, xn_free[s]])
                    done = normalised(s, t, x_n[s][:, t, P:DIM], shifted[s][:, t, :], [stats, xn_free[s]])
                shift_free[s] = [done]
                biased = pool.do(lambda e: e.tensor_tensor(
                    resid[:, b], resid[:, b], bias_row[:, :].unsqueeze(1).to_broadcast([P, TILES, DIM]), ALU.add),
                    [done, added, weights["small"]], "bias")
                resid_done[b] = [biased]
                yield
                ready = to_features(s, lambda t: x_n[s][:, t, :], [done], False, weights["small"])
                xn_free[s] = ready
                act_in = work[s][:, :, :].rearrange("p a n -> p (a n)")
                gate = act_in[:, 0:HC * TOKENS].rearrange("p (m n) -> p m n", m=HC)
                hidden = act_in[:, HC * TOKENS:2 * HC * TOKENS].rearrange("p (m n) -> p m n", m=HC)
                blank = pool.do(lambda e: e.memset(hidden[:, HC - 1, :], 0.0), [o_read], "blank")
                yield

                def up(part, m):
                    n = P if m < HC - 1 else HLAST
                    return [(lambda dst, c=c: mm(dst, w_up[:, c, part * HID + m * P:part * HID + m * P + n],
                                                 x_t[s][:, c, 1:1 + TOKENS], c == 0, c == FC - 1)) for c in range(FC)], n

                for m0 in range(0, HC, 2):
                    tile = wide.take()
                    for m in (m0, m0 + 1):
                        steps, n = up(1, m)
                        dst = tile.buf[0:n, (m - m0) * 512:(m - m0) * 512 + 512]
                        for one in steps:
                            last = pe.do(one(dst), [ready, weights["w_up"], tile.free], "up")
                        got = dve.do(lambda e, m=m, n=n, dst=dst: e.tensor_scalar(
                            gate[0:n, m, :], dst, bias_up[0:n, HC + m:HC + m + 1], None, ALU.add),
                            [last, o_read, weights["small"]], "gate")
                    wide.give(tile, got)
                    yield
                act.do(lambda e: e.activation(gate[:, 0:HC - 1, :], gate[:, 0:HC - 1, :], ACT.Gelu), got, "gelu")
                gated = act.do(lambda e: e.activation(gate[0:HLAST, HC - 1, :], gate[0:HLAST, HC - 1, :], ACT.Gelu),
                               got, "gelu")
                for m0 in range(0, HC, 2):
                    tile = wide.take()
                    for m in (m0, m0 + 1):
                        steps, n = up(0, m)
                        dst = tile.buf[0:n, (m - m0) * 512:(m - m0) * 512 + 512]
                        for one in steps:
                            last = pe.do(one(dst), [ready, tile.free], "up")
                        got = dve.do(lambda e, m=m, n=n, dst=dst: e.scalar_tensor_tensor(
                            out=hidden[0:n, m, :], in0=dst, scalar=bias_up[0:n, m:m + 1], in1=gate[0:n, m, :],
                            op0=ALU.add, op1=ALU.mult), [last, gated, blank], "hidden")
                    wide.give(tile, got)
                    yield
                weight_users["w_up"] = [last]
                tile = wide.take()
                for t in range(TILES):
                    for m in range(HC):
                        last = pe.do(mm(tile.buf[:, t * DIM:(t + 1) * DIM], hidden[:, m, t * P:(t + 1) * P],
                                        w_down[:, m, :], m == 0, m == HC - 1),
                                     [got, tile.free, weights["w_down"]], "down")
                weight_users["w_down"] = [last]
                added = dve.do(lambda e: e.tensor_tensor(flat_resid, tile.buf[:, :], flat_resid, ALU.add),
                               [last, biased], "resid")
                wide.give(tile, added)
                weight_users["small"] = [added, ready]
                resid_done[b] = [added]
                stream_free[s] = [last, got]
                if is_last:
                    back = x_n[s][:, :, :].rearrange("p t f -> p (t f)")
                    loaded = load(back, d["saved"][b], [xn_free[s], saves[b]], f"back{s}")
                    yield
                    added = pool.do(lambda e: e.tensor_tensor(flat_resid, flat_resid, back, ALU.add),
                                    [loaded, added], "resid")
                    xn_free[s] = [added]
                    resid_done[b] = [added]
                yield

            def attention_a(s, b):
                q_t = work[s][:, 0].rearrange("p (c n) -> p c n", c=PAIRS)
                v = work[s][:, 1].rearrange("p (t n) -> p t n", t=TILES)
                o_t = work[s][:, 2].rearrange("p (c n) -> p c n", c=PAIRS)
                k_p = kpad[s][:, :].rearrange("p (c j n) -> p c j n", c=PAIRS, j=2)
                wq = w_in[:, 0:2 * INNER].rearrange("p (c n) -> p c n", c=FC)
                wd = w_in[:, 1024:1024 + FC * RANK].rearrange("p (c n) -> p c n", c=FC)
                wk, wv = w_in[:, 1152:1664], w_in[:, 1664:2176]
                stats = norm_stats(s, lambda t: [resid[:, b, t, :]], [resid_done[b], stream_free[s]])
                for t in range(TILES):
                    done = normalised(s, t, x_n[s][:, t, :], resid[:, b, t, :], [stats, xn_free[s]])
                yield
                ready = to_features(s, lambda t: x_n[s][:, t, :], [done], False)
                xn_free[s] = ready
                yield
                for c0 in range(0, PAIRS, 2):
                    tile = wide.take()
                    for c in (c0, c0 + 1):
                        for k in range(FC):
                            last = pe.do(mm(tile.buf[:, (c - c0) * 512:(c - c0) * 512 + 512], wq[:, k, c * P:(c + 1) * P],
                                            x_t[s][:, k, 1:1 + TOKENS], k == 0, k == FC - 1),
                                         [ready, weights["w_in"], tile.free], "qkv")
                    got_q = act.do(lambda e, c0=c0, tile=tile: e.activation(
                        q_t[:, c0:c0 + 2, :].rearrange("p c n -> p (c n)"), tile.buf[:, :], ACT.Copy, scale=HD ** -0.5),
                        [last, stream_free[s]], "q_t")
                    wide.give(tile, got_q)
                latent = x_n[s][:, 0:2, :].rearrange("p a n -> p (a n)")
                tile = wide.take()
                for k in range(FC):
                    last = pe.do(mm(tile.buf[0:RANK, 0:512], wd[:, k, :], x_t[s][:, k, 1:1 + TOKENS], k == 0, k == FC - 1),
                                 [tile.free], "qkv")
                blank = dve.do(lambda e: e.memset(latent[RANK:P, :], 0.0), ready, "blank")
                got = act.do(lambda e: e.activation(latent[0:RANK, :], tile.buf[0:RANK, 0:512], ACT.Copy),
                             [last, ready], "latent")
                wide.give(tile, got)
                yield
                for c0 in range(0, PAIRS, 2):
                    tile = wide.take()
                    for c in (c0, c0 + 1):
                        last = pe.do(mm(tile.buf[:, (c - c0) * 512:(c - c0) * 512 + 512], wk[:, c * P:(c + 1) * P],
                                        latent, True, True), [got, blank, tile.free], "qkv")
                    for j in range(2):
                        r = slice(64 * j, 64 * j + 64)
                        got_k = dve.do(lambda e, c0=c0, j=j, r=r, tile=tile: e.tensor_copy(
                            k_p[r, c0:c0 + 2, j, :], tile.buf[r, :].rearrange("p (c n) -> p c n", c=2)),
                            [last, stream_free[s], kpad_zero[s]], "k_t")
                    wide.give(tile, got_k)
                    tile = wide.take()
                    for t in (c0, c0 + 1):
                        last = pe.do(mm(tile.buf[:, (t - c0) * 512:(t - c0) * 512 + 512], latent[:, t * P:(t + 1) * P],
                                        wv, True, True), [got, blank, tile.free], "qkv")
                    got_v = act.do(lambda e, c0=c0, tile=tile: e.activation(
                        v[:, c0:c0 + 2, :].rearrange("p c n -> p (c n)"), tile.buf[:, :], ACT.Copy),
                        [last, stream_free[s]], "v")
                    wide.give(tile, got_v)
                    yield
                xn_free[s] = [last]
                weight_users["w_in"] = [last]
                ready = [got_q, got_k, got_v]
                out_marks = []
                for h in range(HEADS):
                    c, j = h // 2, h % 2
                    if j == 0:
                        o_tile = narrow[s].take()
                    prs, st = [], small.take()
                    for t0 in range(0, TILES, 2):
                        tile, pr = wide.take(), probs[s].take()
                        prs.append(pr)
                        for t in (t0, t0 + 1):
                            last = pe.do(mm(tile.buf[:, (t - t0) * 512:(t - t0) * 512 + 512], q_t[:, c, t * P:(t + 1) * P],
                                            k_p[:, c, j, :], True, True), [ready, tile.free], "score")
                        low = dve.do(lambda e, t0=t0, tile=tile: e.tensor_reduce(
                            st.buf[:, t0:t0 + 2], tile.buf[:, :].rearrange("p (t n) -> p t n", t=2), AX, ALU.max,
                            negate=True), [last, st.free], "max")
                        for t in (t0, t0 + 1):
                            cut = slice((t - t0) * 512, (t - t0) * 512 + 512)
                            done = act.do(lambda e, t=t, cut=cut, tile=tile, pr=pr: e.activation(
                                pr.buf[:, cut], tile.buf[:, cut], ACT.Exp, bias=st.buf[:, t:t + 1],
                                accum_out=st.buf[:, 4 + t:5 + t]), [low, pr.free], "exp")
                        wide.give(tile, done)
                    inv = dve.do(lambda e: e.reciprocal(st.buf[:, 8:12], st.buf[:, 4:8]), done, "inv")
                    for t in range(TILES):
                        cut = slice((t % 2) * 512, (t % 2) * 512 + 512)
                        queue = dve if t % 2 else pool
                        scaled = queue.do(lambda e, t=t, cut=cut: e.tensor_scalar(
                            prs[t // 2].buf[:, cut], prs[t // 2].buf[:, cut], st.buf[:, 8 + t:9 + t], 1.0,
                            ALU.mult, ALU.mult), [inv, done], "weight")
                        if t == TILES - 2:
                            scaled_p = scaled
                    scaled = [scaled, scaled_p]
                    small.give(st, scaled)
                    yield
                    for kb0 in range(0, TILES, 2):
                        tile, pt = wide.take(), prob_t.take()
                        for kb in (kb0, kb0 + 1):
                            for t in range(TILES):
                                at = (kb - kb0) * 512 + t * P
                                last = pe.do(tr(tile.buf[:, at:at + P],
                                                prs[t // 2].buf[:, (t % 2) * 512 + kb * P:(t % 2) * 512 + kb * P + P]),
                                             [scaled, tile.free], "turn")
                        got1 = act.do(lambda e, tile=tile, pt=pt: e.activation(pt.buf[:, 0:512], tile.buf[:, 0:512], ACT.Copy),
                                      [last, pt.free], "prob_t")
                        got2 = dve.do(lambda e, tile=tile, pt=pt: e.tensor_copy(pt.buf[:, 512:1024], tile.buf[:, 512:1024]),
                                      [last, pt.free], "prob_t")
                        wide.give(tile, got1, got2)
                        turn_last = last
                        for kb in (kb0, kb0 + 1):
                            last = pe.do(mm(o_tile.buf[64 * j:64 * j + 64, :], v[:, kb, h * HD:(h + 1) * HD],
                                            pt.buf[:, (kb - kb0) * 512:(kb - kb0) * 512 + 512], kb == 0, kb == TILES - 1),
                                         [got1, got2, o_tile.free if j == 0 else []], "mix")
                        prob_t.give(pt, last)
                    for pr in prs:
                        Ring.give(pr, turn_last)
                    if j == 1:
                        done = act.do(lambda e, c=c, o=o_tile: e.activation(o_t[:, c, :], o.buf[:, :], ACT.Copy),
                                      [last, stream_free[s]], "o_t")
                        Ring.give(o_tile, done)
                        out_marks.append(done)
                    yield
                o_read, added = project_out(s, b, lambda c: o_t[:, c, :], PAIRS, out_marks)
                resid_done[b] = [added]
                stream_free[s] = [o_read]
                yield

            def attention_causal(s, b):
                q_a = work[s][:, 0].rearrange("p (g t n) -> p g t n", g=GROUPS, t=TILES)
                k_a = work[s][:, 1].rearrange("p (g t n) -> p g t n", g=GROUPS, t=TILES)
                v = work[s][:, 2].rearrange("p (t n) -> p t n", t=TILES)
                q_rows, qd_rows = (rows[:, i, s * 512:(s + 1) * 512] for i in range(2))
                k_rows = x_n[s][:, 2:4, :].rearrange("p t f -> p (t f)")
                k_p = kpad[s][:, :].rearrange("p (o h n) -> p o h n", o=2, h=4)
                w = w_in[:, 0:FC * 3 * DIM].rearrange("p (c n) -> p c n", c=FC)
                stats = norm_stats(s, lambda t: [resid[:, b, t, :]], [resid_done[b], stream_free[s]])
                for t in range(TILES):
                    done = normalised(s, t, x_n[s][:, t, :], resid[:, b, t, :], [stats, xn_free[s]])
                biased = pool.do(lambda e: e.tensor_tensor(
                    resid[:, b], resid[:, b], bias_row[:, :].unsqueeze(1).to_broadcast([P, TILES, DIM]), ALU.add),
                    [done, resid_done[b], weights["small"]], "bias")
                resid_done[b] = [biased]
                blank = [pool.do(lambda e, i=i: e.memset(work[s][:, i, :], 0.0), stream_free[s], "blank") for i in range(3)]
                rows4 = lambda a: a.rearrange("p g t (h e) -> p (g t) h e", e=BROW)
                pool.do(lambda e: e.memset(rows4(q_a)[:, :, :, BHD + 1:BHD + 2], 1.0), blank, "blank")
                blank = pool.do(lambda e: e.memset(rows4(k_a)[:, :, :, BHD:BHD + 1], 1.0), blank, "blank")
                yield
                ready = to_features(s, lambda t: x_n[s][:, t, :], [done], False)
                xn_free[s] = ready
                yield
                ends = []
                for t in range(TILES):
                    tile = wide.take()
                    for c in range(FC):
                        for lo, n in ((0, 512), (512, 256)):
                            last = pe.do(mm(tile.buf[:, lo:lo + n], x_t[s][:, c, 1 + t * P:1 + (t + 1) * P],
                                            w[:, c, lo:lo + n], c == 0, c == FC - 1),
                                         [ready, weights["w_in"], tile.free], "qkv")
                    row = scratch.take()
                    got = dve.do(lambda e, tile=tile, row=row: e.tensor_tensor(
                        row.buf[:, 0:3 * DIM], tile.buf[:, 0:3 * DIM], qkv_bias, ALU.add),
                        [last, row.free, weights["small"]], "raw")
                    wide.give(tile, got)
                    sq, ss, sk = probs[s].take(), small.take(), small.take()
                    squared = act.do(lambda e, row=row, sq=sq: e.activation(
                        sq.buf[:, 0:2 * DIM], row.buf[:, 0:2 * DIM], ACT.Square), [got, sq.free], "square")
                    for z, one in ((0, ss), (1, sk)):
                        summed = dve.do(lambda e, z=z, one=one, sq=sq: e.tensor_reduce(
                            one.buf[:, 0:16], sq.buf[:, z * DIM:(z + 1) * DIM].rearrange("p (h e) -> p h e", e=BHD),
                            AX, ALU.add), [squared, one.free], "ss")
                    Ring.give(sq, summed)
                    head = lambda a: a.rearrange("p (g h e) -> p g h e", g=GROUPS, e=BHD)
                    slot = lambda a, t, lo, n: a[:, :, t, :].rearrange("p g (h e) -> p g h e", e=BROW)[:, :, :, lo:lo + n]
                    one4 = lambda a: a[:, 0:16].rearrange("p (g h e) -> p g h e", g=GROUPS, e=1)
                    w1 = pool.do(lambda e, t=t, row=row: e.tensor_scalar(slot(q_a, t, 0, BHD), head(row.buf[:, 0:DIM]),
                                                                         -2.0, 1.0, ALU.mult, ALU.mult), [got, blank], "rows")
                    w2 = pool.do(lambda e, t=t, row=row: e.tensor_scalar(slot(k_a, t, 0, BHD), head(row.buf[:, DIM:2 * DIM]),
                                                                         1.0, 1.0, ALU.mult, ALU.mult), [got, blank], "rows")
                    w3 = pool.do(lambda e, t=t, ss=ss: e.tensor_scalar(slot(q_a, t, BHD, 1), one4(ss.buf), EPS_B, 1.0,
                                                                       ALU.add, ALU.mult), [summed, blank], "rows")
                    w4 = pool.do(lambda e, t=t, sk=sk: e.tensor_scalar(slot(k_a, t, BHD + 1, 1), one4(sk.buf), 1.0, 1.0,
                                                                       ALU.mult, ALU.mult), [summed, blank], "rows")
                    w5 = act.do(lambda e, t=t, row=row: e.activation(
                        v[:, t, :].rearrange("p (h e) -> p h e", e=BROW)[:, :, 0:BHD],
                        row.buf[:, 2 * DIM:3 * DIM].rearrange("p (h e) -> p h e", e=BHD), ACT.Copy), [got, blank], "v")
                    scratch.give(row, squared, w4, w5)
                    small.give(ss, w4)
                    small.give(sk, w4)
                    ends = [w4, w5]
                    yield
                weight_users["w_in"] = [last]
                weight_users["small"] = [biased, got]
                out_marks = []
                for g in range(GROUPS):
                    tile = wide.take()
                    for t in range(TILES):
                        pe.do(tr(tile.buf[:, t * P:(t + 1) * P], q_a[:, g, t, :]), [ends, tile.free], "turn")
                        last = pe.do(tr(tile.buf[:, 512 + t * P:512 + (t + 1) * P], k_a[:, g, t, :]), [ends], "turn")
                    a1 = act.do(lambda e, tile=tile: e.activation(q_rows, tile.buf[:, 0:512], ACT.Copy), [last, group_free[s]], "q_t")
                    a2 = act.do(lambda e, tile=tile: e.activation(k_rows, tile.buf[:, 512:1024], ACT.Copy), [last, group_free[s]], "k_t")
                    a3 = dve.do(lambda e, tile=tile: e.tensor_scalar(qd_rows, tile.buf[:, 0:512], dot_rows[:, 0:1], None,
                                                                     ALU.mult), [a1, group_free[s], consts], "q_t")
                    wide.give(tile, a1, a2, a3)
                    turned = last
                    o = g % 2
                    spread = [load(k_p[32 * j:32 * j + 32, o, j, :], k_rows[32 * j:32 * j + 32, :],
                                   [a2, kpad_zero[s], pad_free[s][o]], f"spread{s}") for j in range(4)][-1]
                    yield
                    o_tile = narrow[s].take()
                    for j in range(4):
                        h = 4 * g + j
                        pts = []
                        prs = [probs[s].take(), probs[s].take()]
                        st = small.take()
                        for t in range(TILES):
                            n = P * (t + 1)
                            tile = wide.take()
                            pe.do(mm(tile.buf[:, 0:n], qd_rows[:, t * P:(t + 1) * P], k_p[:, o, j, 0:n], True, True),
                                  [a1, a3, spread, tile.free], "score")
                            last = pe.do(mm(tile.buf[:, 512:512 + n], q_rows[:, t * P:(t + 1) * P], k_p[:, o, j, 0:n],
                                            True, True), [a1, a3, spread], "score")
                            pr = prs[t // 2].buf[:, (t % 2) * 512:(t % 2) * 512 + n]
                            sc = scratch.take()
                            num = act.do(lambda e, sc=sc, tile=tile, n=n: e.activation(
                                sc.buf[:, 0:n], tile.buf[:, 0:n], ACT.Square, scale=0.5), [last, sc.free], "square")
                            den = dve.do(lambda e, sc=sc, tile=tile, n=n: e.reciprocal(
                                sc.buf[:, 512:512 + n], tile.buf[:, 512:512 + n]), [last, sc.free], "inv")
                            wide.give(tile, num, den)
                            div = dve.do(lambda e, sc=sc, n=n: e.tensor_tensor(
                                sc.buf[:, 0:n], sc.buf[:, 0:n], sc.buf[:, 512:512 + n], ALU.mult), [num, den], "ratio")
                            low = dve.do(lambda e, sc=sc, n=n, t=t, pr=pr: e.tensor_tensor_reduce(
                                pr, sc.buf[:, 0:n], causal_mask[:, TOKENS - n:TOKENS],
                                -1.0, LOW, ALU.add, ALU.min, st.buf[:, t:t + 1]), [div, st.free, prs[0].free, prs[1].free, consts], "max")
                            done = act.do(lambda e, sc=sc, n=n, t=t, pr=pr: e.activation(
                                pr, pr, ACT.Exp, bias=st.buf[:, t:t + 1], scale=-1.0,
                                accum_out=st.buf[:, 4 + t:5 + t]), low, "exp")
                            scratch.give(sc, low)
                            if t % 2:
                                yield
                        inv = dve.do(lambda e: e.reciprocal(st.buf[:, 8:12], st.buf[:, 4:8]), done, "inv")
                        for t in range(TILES):
                            pr = prs[t // 2].buf[:, (t % 2) * 512:(t % 2) * 512 + P * (t + 1)]
                            scaled = pool.do(lambda e, t=t, pr=pr: e.tensor_scalar(
                                pr, pr, st.buf[:, 8 + t:9 + t], 1.0, ALU.mult, ALU.mult), [inv, done], "weight")
                        small.give(st, scaled)
                        yield
                        for kb0 in range(0, TILES, 2):
                            tile, pt = wide.take(), prob_t.take()
                            for kb in (kb0, kb0 + 1):
                                for t in range(kb, TILES):
                                    at = (kb - kb0) * 512 + t * P
                                    last = pe.do(tr(tile.buf[:, at:at + P],
                                                    prs[t // 2].buf[:, (t % 2) * 512 + kb * P:(t % 2) * 512 + kb * P + P]),
                                                 [scaled, tile.free], "turn")
                            turn_last = last
                            got1 = act.do(lambda e, tile=tile, pt=pt, k=kb0: e.activation(
                                pt.buf[:, P * k:512], tile.buf[:, P * k:512], ACT.Copy), [last, pt.free], "prob_t")
                            got2 = act.do(lambda e, tile=tile, pt=pt, k=kb0 + 1: e.activation(
                                pt.buf[:, 512 + P * k:1024], tile.buf[:, 512 + P * k:1024], ACT.Copy), [last, pt.free], "prob_t")
                            wide.give(tile, got1, got2)
                            for kb in (kb0, kb0 + 1):
                                last = pe.do(mm(o_tile.buf[32 * j:32 * j + 32, P * kb:512], v[:, kb, h * BROW:(h + 1) * BROW],
                                                pt.buf[:, (kb - kb0) * 512 + P * kb:(kb - kb0) * 512 + 512],
                                                kb == 0, kb == TILES - 1), [got1, got2, o_tile.free], "mix")
                            prob_t.give(pt, last)
                        Ring.give(prs[0], turn_last)
                        Ring.give(prs[1], turn_last)
                        pad_free[s][o] = [last]
                        group_free[s] = [last]
                        xn_free[s] = [last]
                        yield
                    out = q_a[:, g].rearrange("p t n -> p (t n)")
                    done = act.do(lambda e, out=out, o_tile=o_tile: e.activation(out, o_tile.buf[:, :], ACT.Copy),
                                  [last, turned], "o_t")
                    Ring.give(o_tile, done)
                    out_marks.append(done)
                o_read, added = project_out(s, b, lambda c: q_a[:, c].rearrange("p t n -> p (t n)"), GROUPS, out_marks)
                resid_done[b] = [added]
                stream_free[s] = [o_read]
                yield

            rows_free = {"raw": [], "sin": []}
            probs = [None, None]
            shift_free, xn_free, group_free = [[], []], [[], []], [[], []]
            pad_free = [[[], []], [[], []]]
            saves = {}
            kpad_zero = [[], []]
            qkv_bias = w_in[:, 2304:2304 + 3 * DIM]

            def load_weights(stage, depth):
                free = weight_users
                if stage == "a":
                    pads = dve.do(lambda e: e.memset(w_in[RANK:P, 1152:2176], 0.0), free["w_in"], "wpad")
                    load(w_in[:, 0:1024].rearrange("p (c n) -> p c n", c=FC), d["a_wq_t"].rearrange("(c p) n -> p c n", p=P), free["w_in"], "w_in")
                    load(w_in[:, 1024:1152].rearrange("p (c n) -> p c n", c=FC), d["a_wd_t"].rearrange("(c p) n -> p c n", p=P), free["w_in"], "w_in")
                    load(w_in[0:RANK, 1152:1664], d["a_wk_t"], free["w_in"], "w_in")
                    weights["w_in"] = [load(w_in[0:RANK, 1664:2176], d["a_wv_t"], free["w_in"], "w_in"), pads]
                    weights["w_out"] = [load(w_out[:, :].rearrange("p (c n) -> p c n", c=PAIRS),
                                             d["a_wo_t"].rearrange("(c p) n -> p c n", p=P), free["w_out"], "w_out")]
                elif stage == "b":
                    load(w_in[:, 0:FC * 3 * DIM].rearrange("p (c n) -> p c n", c=FC), d["b_wqkv"].rearrange("(c p) n -> p c n", p=P), free["w_in"], "w_in")
                    last = load(w_in[:, 2304:2304 + 3 * DIM], d["b_bqkv"].unsqueeze(0).to_broadcast([P, 3 * DIM]), free["w_in"], "w_in")
                    weights["w_in"] = [last]
                    zero = pool.do(lambda e: e.memset(w_out[:, :], 0.0), free["w_out"], "wpad")
                    for j in range(4):
                        last2 = load(w_out[32 * j:32 * j + BHD, :].rearrange("p (g n) -> p g n", g=GROUPS),
                                     d["b_wout"].rearrange("(g j e) n -> j e g n", g=GROUPS, e=BHD)[j], zero, "w_out")
                    weights["w_out"] = [last2]
                    weights["small"] = [load(bias_row[:, :], d["b_bout"].unsqueeze(0).to_broadcast([P, DIM]), free["small"], "w_small"), last]
                else:
                    weights["w_in"] = [load(w_in[:, :].rearrange("p (c n) -> p c n", c=FC), d["f_wqkv"][depth].rearrange("(c p) n -> p c n", p=P), free["w_in"], "w_in")]
                    weights["w_out"] = [load(w_out[:, :].rearrange("p (c n) -> p c n", c=PAIRS), d["f_wo"][depth].rearrange("(c p) n -> p c n", p=P), free["w_out"], "w_out")]
                    weights["w_up"] = [load(w_up[:, :, :], d["f_w1"][depth].rearrange("(c p) n -> p c n", p=P), free["w_up"], "w_up")]
                    zero = pool.do(lambda e: e.memset(w_down[:, HC - 1, :], 0.0), free["w_down"], "wpad")
                    load(w_down[:, 0:HC - 1, :], d["f_w2"][depth, 0:(HC - 1) * P].rearrange("(c p) n -> p c n", p=P), free["w_down"], "w_down")
                    weights["w_down"] = [load(w_down[0:HLAST, HC - 1, :], d["f_w2"][depth, (HC - 1) * P:HID], zero, "w_down")]
                    f = free["small"]
                    load(rot[:, :, :, :], d["rotary"], f, "w_small")
                    load(qk_scale[:, 0, :], d["f_qs"][depth].unsqueeze(0).to_broadcast([P, HD]), f, "w_small")
                    load(qk_scale[:, 1, :], d["f_ks"][depth].unsqueeze(0).to_broadcast([P, HD]), f, "w_small")
                    load(ln_gb[:, 0, :], d["f_lg"][depth].rearrange("(c p) -> p c", p=P), f, "w_small")
                    load(ln_gb[:, 1, :], d["f_lb"][depth].rearrange("(c p) -> p c", p=P), f, "w_small")
                    for part in range(2):
                        lo = part * HID
                        load(bias_up[:, part * HC:part * HC + HC - 1],
                             d["f_b1"][depth, lo:lo + (HC - 1) * P].rearrange("(c p) -> p c", p=P), f, "w_small")
                        load(bias_up[0:HLAST, part * HC + HC - 1:part * HC + HC],
                             d["f_b1"][depth, lo + (HC - 1) * P:lo + HID].unsqueeze(1), f, "w_small")
                    last = load(bias_row[:, :], d["f_b2"][depth].unsqueeze(0).to_broadcast([P, DIM]), f, "w_small")
                    for z in range(2):
                        whole = qk_scale[:, z, :].unsqueeze(1).to_broadcast([P, TILES, HD])
                        swap = qk_scale[:, z, :].rearrange("p (u e) -> p u e", u=2)[:, ::-1, :].unsqueeze(1).to_broadcast([P, TILES, 2, HD // 2])
                        pool.do(lambda e, z=z, whole=whole: e.tensor_tensor(rot[:, 2 * z], rot[:, 2 * z], whole, ALU.mult), last, "tables")
                        table = rot[:, 2 * z + 1].rearrange("p t (u e) -> p t u e", u=2)
                        made = pool.do(lambda e, table=table, swap=swap: e.tensor_tensor(table, table, swap, ALU.mult), last, "tables")
                    weights["small"] = [made, last]

            def interleave(units):
                waiting = list(units)
                flying = []
                slots = [0, 1]
                while waiting or flying:
                    while waiting and slots:
                        s = slots.pop(0)
                        flying.append((s, waiting.pop(0)(s)))
                    for item in list(flying):
                        if next(item[1], "end") == "end":
                            flying.remove(item)
                            slots.append(item[0])

            def zero_pads():
                for s in range(2):
                    kpad_zero[s] = [pool.do(lambda e, s=s: e.memset(kpad[s][:, :], 0.0), stream_free[s] + pad_free[s][0] + pad_free[s][1], "kpad")]

            prob_last = [[], []]
            zero_pads()
            for stage, depth in PLAN:
                if stage == "f":
                    for s in range(2):
                        probs[s] = Ring([prob_own[s]])
                else:
                    spare = w_up[:, :, :].rearrange("p c n -> p (c n)")
                    for s in range(2):
                        probs[s] = Ring([prob_own[s], spare[:, s * 1024:(s + 1) * 1024]])
                        probs[s].slots[1].free = list(weight_users["w_up"])
                for s in range(2):
                    probs[s].slots[0].free = list(prob_last[s])
                load_weights(stage, depth)
                if stage == "a":
                    interleave([lambda s, b=b: attention_a(s, b) for b in range(SEQS)])
                elif stage == "b":
                    zero_pads()
                    interleave([lambda s, b=b: attention_causal(s, b) for b in range(SEQS)])
                    zero_pads()
                else:
                    interleave([lambda s, b=b: local_layer(s, b, depth, depth == 0, depth == DEPTH - 1) for b in range(SEQS)])
                for s in range(2):
                    prob_last[s] = probs[s].slots[0].free
                if stage != "f":
                    weight_users["w_up"] = probs[0].slots[1].free + probs[1].slots[1].free
            stored = [sp.do(lambda e, b=b: e.dma_start(d["out"][b].rearrange("(t p) f -> p t f", p=P), resid[:, b]),
                            resid_done[b], "out", 16) for b in range(SEQS)]
            sp.wait(stored[-1])

        block = stack.enter_context(nc.Block())
        for live in ("tensor", "scalar", "vector", "gpsimd", "sync"):
            engine_block = {"tensor": block.tensor, "scalar": block.scalar, "vector": block.vector,
                            "gpsimd": block.gpsimd, "sync": block.sync}[live]
            engine_block(lambda eng, live=live: schedule(live, eng))


PLAN = [("a", 0), ("f", 0), ("f", 1), ("b", 0), ("f", 0), ("f", 1)]


def constants():
    half = np.arange(0, HD, 2, dtype=np.float32)
    inv_freq = (1.0 / np.float32(10000.0) ** (half / np.float32(HD))).astype(np.float32)
    t = np.arange(TOKENS, dtype=np.float32)
    freqs = (t[:, None] * inv_freq[None, :]).astype(np.float32)
    freqs = np.concatenate([freqs, freqs], axis=-1)
    base = (half + 0.4 * HD) / (1.4 * HD)
    power = (t - TOKENS // 2) / float(WINDOW // 2)
    scale = base[None, :].astype(np.float64) ** power[:, None].astype(np.float64)
    scale = np.concatenate([scale, scale], axis=-1)
    cos, sin = np.cos(freqs.astype(np.float64)), np.sin(freqs.astype(np.float64))
    sign = np.where(np.arange(HD) < HD // 2, -1.0, 1.0)
    tables = [8.0 * cos * scale, 8.0 * sin * sign * scale, cos / scale, sin * sign / scale]
    rotary = np.stack([x.reshape(TILES, P, HD) for x in tables]).transpose(2, 0, 1, 3)
    i, j = np.arange(P)[:, None], np.arange(P)[None, :]
    own = np.where(j > i, MASKED, 0.0)
    previous = np.where(j < i, MASKED, 0.0)
    return {
        "ident": np.eye(P), "rotary": rotary,
        "local_mask": np.concatenate([previous, own], axis=1),
        "causal_mask": np.concatenate([np.zeros((P, TOKENS - P)), own], axis=1),
        "dot_rows": (np.arange(P)[:, None] % BROW < BHD) * 1.0,
    }


WINDOW = 128


def kernel(**inputs):
    import concourse.bacc as bacc
    from concourse.bass_utils import run_bass_kernel_spmd

    given = {k: np.asarray(v) for k, v in inputs.items()}
    a, bb, f = "L0_attn_a_", "L0_attn_b_", "L0_ffn_"
    arrays = {
        "x": given[a + "x"], "a_wq_t": given[a + "Wq"].T, "a_wd_t": given[a + "Wkv_down"].T,
        "a_wk_t": given[a + "Wk_up"].T, "a_wv_t": given[a + "Wv_up"].T, "a_wo_t": given[a + "Wo"].T,
        "b_wqkv": given[bb + "w_qkv"], "b_bqkv": given[bb + "b_qkv"], "b_wout": given[bb + "w_out"],
        "b_bout": given[bb + "b_out"], "f_wqkv": given[f + "wqkv"], "f_qs": given[f + "q_scale"],
        "f_ks": given[f + "k_scale"], "f_wo": given[f + "wo"], "f_lg": given[f + "ln_g"], "f_lb": given[f + "ln_b"],
        "f_w1": given[f + "w1"], "f_b1": given[f + "b1"], "f_w2": given[f + "w2"], "f_b2": given[f + "b2"],
    }
    arrays.update({k: v.astype(np.float32) for k, v in constants().items()})
    arrays = {"in_" + k: np.ascontiguousarray(v) for k, v in arrays.items()}
    nc = bacc.Bacc("TRN2", target_bir_lowering=False, num_devices=1)
    d = {k[3:]: nc.dram_tensor(k, v.shape, F32, kind="ExternalInput").ap() for k, v in arrays.items()}
    d["out"] = nc.dram_tensor("out", (SEQS, TOKENS, DIM), F32, kind="ExternalOutput").ap()
    d["saved"] = nc.dram_tensor("saved", (SEQS, P, TILES * DIM), F32).ap()
    build(nc, d)
    result = run_bass_kernel_spmd(nc, [arrays], core_ids=[0])
    return result.results[0]["out"]
```

```python
from contextlib import ExitStack

import numpy as np

import concourse.bass as bass
from concourse import mybir

F32 = mybir.dt.float32
ALU = mybir.AluOpType
ACT = mybir.ActivationFunctionType
AX = mybir.AxisListType.X

P = 128
SEQS, TOKENS, DIM = 8, 512, 256
TILES = TOKENS // P
FC = DIM // P
HEADS, HD = 8, 64
INNER = HEADS * HD
PAIRS = HEADS // 2
RANK = 64
BHEADS, BHD, BROW = 16, 16, 32
GROUPS = BHEADS * BROW // P
HID = int(DIM * 4 * 2 / 3)
HC = -(-HID // P)
HLAST = HID - (HC - 1) * P
DEPTH = 2
EPS_LN, EPS_B = 1e-5, 1e-6
MASKED = -1e30
LOW = 3e38


class Mark:

    def __init__(self, sem, value):
        self.sem, self.value = sem, value


class Signals:

    def __init__(self, nc, stack):
        self.nc, self.stack, self.sems, self.counts = nc, stack, {}, {}

    def restart(self):
        self.counts = {}

    def count(self, name, step):
        if name not in self.sems:
            self.sems[name] = self.stack.enter_context(self.nc.semaphore("s_" + name))
        self.counts[name] = self.counts.get(name, 0) + step
        return Mark(self.sems[name], self.counts[name])


class Queue:

    def __init__(self, name, signals, eng):
        self.name, self.signals, self.eng, self.seen = name, signals, eng, {}

    def do(self, emit, waits=(), signal="done", step=1):
        mark = self.signals.count(f"{self.name}_{signal}", step)
        if self.eng is not None:
            self.wait(waits)
            emit(self.eng).then_inc(mark.sem, step)
        return mark

    def wait(self, waits):
        if self.eng is None:
            return
        for mark in flat(waits):
            if self.seen.get(id(mark.sem), 0) < mark.value:
                self.seen[id(mark.sem)] = mark.value
                self.eng.wait_ge(mark.sem, mark.value)


def flat(waits):
    if isinstance(waits, Mark):
        return [waits]
    return [m for w in waits for m in flat(w)]


class Slot:

    def __init__(self, buf):
        self.buf, self.free, self.taken = buf, [], False


class Ring:

    def __init__(self, bufs):
        self.slots, self.next = [Slot(b) for b in bufs], 0

    def take(self):
        slot = self.slots[self.next % len(self.slots)]
        assert not slot.taken, "a ring's buffer is still in use"
        slot.taken = True
        self.next += 1
        return slot

    @staticmethod
    def give(slot, *marks):
        slot.free, slot.taken = list(marks), False


def build(nc, d):
    stack = ExitStack()
    with stack:
        sig = Signals(nc, stack)
        def sb(name, *shape):
            return stack.enter_context(nc.sbuf_tensor(name, [P, *shape], F32))

        resid = sb("resid", SEQS, TILES, DIM)
        w_in = sb("w_in", 3072)
        w_out = sb("w_out", 1024)
        w_up = sb("w_up", FC, 2 * HID)
        w_down = sb("w_down", HC, DIM)
        rot = sb("rot", 4, TILES, HD)
        qk_scale = sb("qk_scale", 2, HD)
        ln_gb = sb("ln_gb", 2, FC)
        bias_up = sb("bias_up", 2 * HC)
        bias_row = sb("bias_row", DIM)
        ident = sb("ident", P)
        local_mask = sb("local_mask", 2 * P)
        causal_mask = sb("causal_mask", P)
        minus_half = sb("minus_half", 64)
        dot_rows = sb("dot_rows", 1)
        work = [sb(f"work{s}", 3, 4 * TOKENS) for s in range(2)]
        kpad = [sb(f"kpad{s}", 8 * TOKENS) for s in range(2)]
        x_t = [sb(f"x_t{s}", FC, TOKENS + 1) for s in range(2)]
        x_n = [sb(f"x_n{s}", TILES, DIM) for s in range(2)]
        shifted = [sb(f"shifted{s}", TILES, P) for s in range(2)]
        stat = [sb(f"stat{s}", 256) for s in range(2)]
        rows = sb("rows", 2, 2 * TOKENS)
        scratch_buf = sb("scratch", 2 * TOKENS)
        prob_own = [sb(f"prob{s}", 2 * TOKENS) for s in range(2)]
        prob_t_bufs = [sb(f"prob_t{i}", 2 * TOKENS) for i in range(2)]
        small_bufs = [sb(f"small{i}", 16) for i in range(16)]

        wide_bufs = [stack.enter_context(nc.psum_tensor(f"wide{i}", [P, 1024], F32)) for i in range(3)]
        narrow_bufs = [stack.enter_context(nc.psum_tensor(f"narrow{i}", [P, 512], F32)) for i in range(2)]

        def schedule(live, eng):
            sig.restart()
            pe, act, dve, pool, sp = (Queue(n, sig, eng if n2 == live else None) for n, n2 in (
                ("pe", "tensor"), ("act", "scalar"), ("dve", "vector"), ("pool", "gpsimd"), ("sp", "sync")))
            small = Ring(small_bufs)
            scratch = [Slot(scratch_buf[:, 0:512]), Slot(scratch_buf[:, 512:1024])]
            prob_t = [Ring([buf]) for buf in prob_t_bufs]
            wide = Ring(wide_bufs)
            narrow = [Ring([buf]) for buf in narrow_bufs]
            def load(dst, src, waits, signal):
                return sp.do(lambda e: e.dma_start(dst, src, allow_slow_non_contiguous=True), waits, signal, 16)

            consts = [
                load(ident[:, :], d["ident"], [], "const"),
                load(local_mask[:, :], d["local_mask"], [], "const"),
                load(causal_mask[:, :], d["causal_mask"], [], "const"),
                load(dot_rows[:, :], d["dot_rows"], [], "const"),
            ][-1]
            consts = [consts, pool.do(lambda e: e.memset(minus_half[:, :], -0.5), [], "zero")]
            arrived = [load(resid[:, b], d["x"][b].rearrange("(t p) f -> p t f", p=P), [], f"x{b}")
                       for b in range(SEQS)]
            resid_done = [[m] for m in arrived]
            for s in range(2):
                first = pool.do(lambda e, s=s: e.memset(x_t[s][:, :, 0:1], 0.0), [], "zero")
                first = pool.do(lambda e, s=s: e.memset(shifted[s][:, :, :], 0.0), [], "zero")
                consts.append(first)

            weights = {}
            weight_users = {k: {} for k in ("w_in", "w_out", "w_up", "w_down", "small")}
            stream_free = [[], []]

            def mm(out, lhsT, rhs, start, stop, **k):
                return lambda e: e.matmul(out, lhsT, rhs, start=start, stop=stop, skip_group_check=True, **k)

            def tr(out, in_):
                return lambda e: e.transpose(out, in_, ident[0:in_.shape[0], 0:in_.shape[0]])

            def norm_stats(s, pieces, waits):
                st = stat[s]
                n = len(pieces(0))
                for t in range(TILES):
                    for i, piece in enumerate(pieces(t)):
                        got = dve.do(lambda e, t=t, i=i, piece=piece: e.bn_stats(
                            st[:, (t * 2 + i) * 6:(t * 2 + i) * 6 + 6], piece), waits, "stat")
                for t in range(TILES):
                    got = dve.do(lambda e, t=t: e.bn_aggr(
                        st[:, 64 + 2 * t:66 + 2 * t], st[:, t * 12:t * 12 + 6 * n]), got, "stat")
                var = st[:, 64:64 + 2 * TILES].rearrange("p (t c) -> p t c", c=2)[:, :, 1]
                eps = dve.do(lambda e: e.tensor_scalar(st[:, 80:80 + TILES], var, EPS_LN, None, ALU.add), got, "stat")
                power = pool.do(lambda e: e.tensor_tensor(st[:, 96:96 + TILES], st[:, 80:80 + TILES],
                                                          minus_half[:, 0:TILES], ALU.pow), [eps, consts], "rstd")
                return [got, power]

            def normalised(s, t, dst, src, waits):
                st = stat[s]
                return dve.do(lambda e: e.tensor_scalar(dst, src, st[:, 64 + 2 * t:65 + 2 * t],
                                                        st[:, 96 + t:97 + t], ALU.subtract, ALU.mult), waits, "norm")

            def to_features(s, src, waits, shift, scaled=None):
                done = []
                tile = wide.take()
                for c in range(FC):
                    for t in range(TILES):
                        last = pe.do(tr(tile.buf[:, c * TOKENS + t * P:c * TOKENS + (t + 1) * P],
                                        src(t)[:, c * P:(c + 1) * P]), [waits, tile.free, consts], "turn")
                for c in range(FC):
                    dst = x_t[s][:, c, 1:1 + TOKENS]
                    ps = tile.buf[:, c * TOKENS:(c + 1) * TOKENS]
                    if scaled is None:
                        done.append(act.do(lambda e, dst=dst, ps=ps: e.activation(dst, ps, ACT.Copy),
                                           [last, stream_free[s]], "x_t"))
                    else:
                        done.append(dve.do(lambda e, dst=dst, ps=ps, c=c: e.tensor_scalar(
                            dst, ps, ln_gb[:, 0, c:c + 1], ln_gb[:, 1, c:c + 1], ALU.mult, ALU.add),
                            [last, stream_free[s], scaled], "x_t"))
                wide.give(tile, done)
                return done

            def project_out(s, b, out_t, chunks, rows_done, extra=None):
                tile = wide.take()
                for t in range(TILES):
                    for c in range(chunks):
                        last = pe.do(mm(tile.buf[:, t * DIM:(t + 1) * DIM], out_t(c)[:, t * P:(t + 1) * P],
                                        w_out[:, c * DIM:(c + 1) * DIM], c == 0, c == chunks - 1),
                                     [rows_done, tile.free, weights["w_out"]], "proj")
                dst = resid[:, b].rearrange("p t f -> p (t f)")
                added = dve.do(lambda e: e.tensor_tensor(dst, tile.buf[:, :], dst, ALU.add), [last, resid_done[b]], "resid")
                wide.give(tile, added)
                finish("w_out", s, last)
                return last, added

            def in_turns(steps, softmax, normalise, turn, mix, prepare=None):
                steps = list(steps)
                weighed = turned = None
                for k in range(len(steps) + 2):
                    if k < len(steps) and prepare is not None and prepare(steps[k]) is not None:
                        yield
                    scored = softmax(steps[k]) if k < len(steps) else None
                    yield
                    if turned is not None:
                        mix(*turned)
                    turned = turn(*weighed) if weighed is not None else None
                    yield
                    weighed = normalise(*scored) if scored is not None else None
                    yield

            def local_layer(s, b, stage, is_first, is_last):
                q_t = work[s][:, 0].rearrange("p (c n) -> p c n", c=PAIRS)
                v = work[s][:, 1].rearrange("p (t n) -> p t n", t=TILES)
                o_t = work[s][:, 2].rearrange("p (c n) -> p c n", c=PAIRS)
                k_p = kpad[s][:, :].rearrange("p (c j n) -> p c j n", c=PAIRS, j=2)
                flat_resid = resid[:, b].rearrange("p t f -> p (t f)")
                zero_pads(s, "pairs")
                if is_first:
                    saved = sp.do(lambda e: e.dma_start(d["saved"][b], flat_resid), resid_done[b], f"saved{b}", 16)
                    stats = norm_stats(s, lambda t: [resid[:, b, t, :]], [resid_done[b], stream_free[s]])
                    yield
                    for t in range(TILES):
                        done = normalised(s, t, resid[:, b, t, :], resid[:, b, t, :], [stats, saved])
                    resid_done[b] = [done]
                    saves[b] = saved
                    yield
                ready = to_features(s, lambda t: resid[:, b, t, :], [resid_done[b]], True)
                yield
                yield from claim("w_in", stage)
                yield from claim("small", stage)
                heads = lambda a: a.rearrange("p (h e) -> p h e", e=HD)
                halves = lambda a: a.rearrange("p (h u e) -> p h u e", u=2, e=HD // 2)
                final = Ring([x_n[s][:, :, :].rearrange("p t f -> p (t f)"), prob_own[s][:, :]])
                final.slots[0].free, final.slots[1].free = xn_free[s], prob_free[s]

                def rotated(t):
                    raw, sines = rows[:, 0, :], rows[:, 1, :]
                    out, tile, vtile = final.take(), wide.take(), wide.take()
                    for third, dst in ((0, tile.buf[:, 0:512]), (1, tile.buf[:, 512:1024]), (2, vtile.buf[:, 0:512])):
                        for c in range(FC):
                            last = pe.do(mm(dst, x_t[s][:, c, 1 - c + t * P:1 - c + (t + 1) * P],
                                            w_in[:, c * 3 * INNER + third * INNER:c * 3 * INNER + (third + 1) * INNER],
                                            c == 0, c == FC - 1),
                                         [ready, weights["w_in"], tile.free, vtile.free], "qkv")
                    copied = act.do(lambda e: e.activation(raw, tile.buf[:, :], ACT.Copy),
                                    [last, rows_free["raw"]], "raw")
                    squared = act.do(lambda e: e.activation(scratch_buf[:, :], tile.buf[:, :], ACT.Square),
                                     [last, scratch[0].free, scratch[1].free], "square")
                    got_v = act.do(lambda e: e.activation(v[:, t, :], vtile.buf[:, 0:512], ACT.Copy),
                                   [last, stream_free[s]], "v")
                    wide.give(tile, squared)
                    wide.give(vtile, got_v)
                    for z in range(2):
                        part = slice(z * INNER, (z + 1) * INNER)
                        sind = pool.do(lambda e: e.tensor_tensor(
                            halves(sines[:, part]), halves(raw[:, part])[:, :, ::-1, :],
                            rot[:, 2 * z + 1, t, :].rearrange("p (u e) -> p u e", u=2).unsqueeze(1)
                            .to_broadcast([P, HEADS, 2, HD // 2]), ALU.mult),
                            [copied, rows_free["sin"], weights["small"]], "sin")
                        cosd = dve.do(lambda e: e.tensor_tensor(
                            heads(out.buf[:, part]), heads(raw[:, part]),
                            rot[:, 2 * z, t, :].unsqueeze(1).to_broadcast([P, HEADS, HD]), ALU.mult),
                            [copied, out.free, weights["small"]], "cos")
                    rows_free["raw"] = [sind, cosd]
                    ss, rn = small.take(), small.take()
                    summed = dve.do(lambda e: e.tensor_reduce(ss.buf[:, 0:16], heads(scratch_buf[:, :]), AX, ALU.add),
                                    [squared, ss.free], "ss")
                    scratch[0].free = scratch[1].free = [summed]
                    clipped = dve.do(lambda e: e.tensor_scalar(ss.buf[:, 0:16], ss.buf[:, 0:16], 1e-24, None, ALU.max),
                                     summed, "ss")
                    power = pool.do(lambda e: e.tensor_tensor(rn.buf[:, 0:16], ss.buf[:, 0:16], minus_half[:, 0:16],
                                                              ALU.pow), [clipped, rn.free, consts], "rn")
                    small.give(ss, power)
                    return t, out, rn, sind, cosd, power, got_v, last

                def joined(t, out, rn, sind, cosd, power, got_v, last):
                    sines = rows[:, 1, :]
                    total = dve.do(lambda e: e.tensor_tensor(out.buf[:, :], out.buf[:, :], sines, ALU.add),
                                   [cosd, sind], "turned")
                    rows_free["sin"] = [total]
                    scaled = pool.do(lambda e: e.tensor_tensor(
                        heads(out.buf[:, :]), heads(out.buf[:, :]), rn.buf[:, 0:16].unsqueeze(2)
                        .to_broadcast([P, 16, HD]), ALU.mult), [total, power], "scaled")
                    small.give(rn, scaled)
                    return t, out, scaled, got_v

                def spread_out(t, out, scaled, got_v):
                    tile = wide.take()
                    for z in range(8):
                        last = pe.do(tr(tile.buf[:, z * P:(z + 1) * P], out.buf[:, z * P:(z + 1) * P]),
                                     [scaled, tile.free], "turn")
                    final.give(out, last)
                    packed = tile.buf[:, :].rearrange("p (z c n) -> p z c n", z=2, c=PAIRS)
                    got_q = act.do(lambda e: e.activation(q_t[:, :, t * P:(t + 1) * P], packed[:, 0], ACT.Copy),
                                   [last, stream_free[s]], "q_t")
                    for j in range(2):
                        r = slice(64 * j, 64 * j + 64)
                        got_k = dve.do(lambda e: e.tensor_copy(k_p[r, :, j, t * P:(t + 1) * P], packed[r, 1]),
                                       [last, stream_free[s], kpad_zero[s]], "k_t")
                    wide.give(tile, got_q, got_k)
                    return [got_q, got_k, got_v]

                ready_out, before = [], None
                for t in range(TILES + 1):
                    now = rotated(t) if t < TILES else None
                    if now is not None:
                        last_in = now[-1]
                        now = joined(*now)
                    yield
                    if before is not None:
                        ready_out = spread_out(*before)
                        yield
                    before = now
                finish("w_in", s, last_in)
                prob_free[s], xn_free[s] = final.slots[1].free, final.slots[0].free
                ready = ready_out
                out_marks = []
                held = Ring([prob_own[s], x_n[s][:, :, :].rearrange("p t f -> p (t f)")])
                held.slots[0].free, held.slots[1].free = prob_free[s], xn_free[s]
                span = lambda t: slice(256 * t + (P if t == 0 else 0), 256 * (t + 1))

                def softmax(h):
                    c, j = h // 2, h % 2
                    tile, st, pr = wide.take(), small.take(), held.take()
                    for t in range(TILES):
                        last = pe.do(mm(tile.buf[:, span(t)], q_t[:, c, t * P:(t + 1) * P],
                                        k_p[:, c, j, P * max(t - 1, 0):(t + 1) * P], True, True),
                                     [ready, tile.free], "score")
                    for t in range(TILES):
                        low = dve.do(lambda e: e.tensor_tensor_reduce(
                            pr.buf[:, span(t)], tile.buf[:, span(t)], local_mask[:, P if t == 0 else 0:256],
                            -1.0, LOW, ALU.add, ALU.min, st.buf[:, t:t + 1]),
                            [last, pr.free, st.free, consts], "max")
                        done = act.do(lambda e: e.activation(
                            pr.buf[:, span(t)], pr.buf[:, span(t)], ACT.Exp, bias=st.buf[:, t:t + 1], scale=-1.0,
                            accum_out=st.buf[:, 4 + t:5 + t]), low, "exp")
                    wide.give(tile, low)
                    return h, pr, st, done

                def normalise(h, pr, st, done):
                    inv = dve.do(lambda e: e.reciprocal(st.buf[:, 8:12], st.buf[:, 4:8]), done, "inv")
                    for t in range(TILES):
                        scaled = pool.do(lambda e: e.tensor_scalar(
                            pr.buf[:, span(t)], pr.buf[:, span(t)], st.buf[:, 8 + t:9 + t], 1.0,
                            ALU.mult, ALU.mult), [inv, done], "weight")
                    small.give(st, scaled)
                    return h, pr, scaled

                def turn(h, pr, scaled):
                    tile, pt = wide.take(), prob_t[s].take()
                    for kb in range(TILES):
                        for t in range(kb, min(kb + 2, TILES)):
                            col = 256 * t + (P if t == kb else 0)
                            last = pe.do(tr(tile.buf[:, 256 * kb + P * (t - kb):256 * kb + P * (t - kb + 1)],
                                            pr.buf[:, col:col + P]), [scaled, tile.free], "turn")
                    held.give(pr, last)
                    got1 = act.do(lambda e: e.activation(pt.buf[:, 0:512], tile.buf[:, 0:512], ACT.Copy),
                                  [last, pt.free], "prob_t")
                    got2 = dve.do(lambda e: e.tensor_copy(pt.buf[:, 512:896], tile.buf[:, 512:896]),
                                  [last, pt.free], "prob_t")
                    wide.give(tile, got1, got2)
                    return h, pt, [got1, got2]

                def mix(h, pt, turned):
                    c, j = h // 2, h % 2
                    if j == 0:
                        o_tiles.append(narrow[s].take())
                    o_tile = o_tiles[-1]
                    for kb in range(TILES):
                        n = P * min(2, TILES - kb)
                        last = pe.do(mm(o_tile.buf[64 * j:64 * j + 64, P * kb:P * kb + n],
                                        v[:, kb, h * HD:(h + 1) * HD], pt.buf[:, 256 * kb:256 * kb + n],
                                        kb == 0, kb == TILES - 1), [turned, o_tile.free], "mix")
                    prob_t[s].give(pt, last)
                    if j == 1:
                        done = act.do(lambda e: e.activation(o_t[:, c, :], o_tile.buf[:, :], ACT.Copy),
                                      [last, stream_free[s]], "o_t")
                        narrow[s].give(o_tile, done)
                        out_marks.append(done)

                o_tiles = []
                yield from in_turns(range(HEADS), softmax, normalise, turn, mix)
                prob_free[s], xn_free[s] = held.slots[0].free, held.slots[1].free
                yield from claim("w_out", stage)
                o_read, added = project_out(s, b, lambda c: o_t[:, c, :], PAIRS, out_marks)
                resid_done[b] = [added]
                yield
                moved = [
                    sp.do(lambda e: e.dma_start(shifted[s][1:P, :, :], resid[0:P - 1, b, :, P:DIM]),
                          [added, shift_free[s]], f"shift{s}", 16),
                    sp.do(lambda e: e.dma_start(shifted[s][0:1, 1:TILES, :], resid[P - 1:P, b, 0:TILES - 1, P:DIM]),
                          [added, shift_free[s]], f"shift{s}", 16)]
                stats = norm_stats(s, lambda t: [resid[:, b, t, 0:P], shifted[s][:, t, :]], [added, moved[-1], consts])
                yield
                for t in range(TILES):
                    normalised(s, t, x_n[s][:, t, 0:P], resid[:, b, t, 0:P], [stats, xn_free[s]])
                    done = normalised(s, t, x_n[s][:, t, P:DIM], shifted[s][:, t, :], [stats, xn_free[s]])
                shift_free[s] = [done]
                biased = pool.do(lambda e: e.tensor_tensor(
                    resid[:, b], resid[:, b], bias_row[:, :].unsqueeze(1).to_broadcast([P, TILES, DIM]), ALU.add),
                    [done, added, weights["small"]], "bias")
                resid_done[b] = [biased]
                yield
                ready = to_features(s, lambda t: x_n[s][:, t, :], [done], False, weights["small"])
                xn_free[s] = ready
                act_in = work[s][:, :, :].rearrange("p a n -> p (a n)")
                gate = act_in[:, 0:HC * TOKENS].rearrange("p (m n) -> p m n", m=HC)
                hidden = act_in[:, HC * TOKENS:2 * HC * TOKENS].rearrange("p (m n) -> p m n", m=HC)
                blank = pool.do(lambda e: e.memset(hidden[:, HC - 1, :], 0.0), [o_read], "blank")
                yield

                yield from claim("w_up", stage)

                def up(part, m):
                    n = P if m < HC - 1 else HLAST
                    return [(lambda dst, c=c: mm(dst, w_up[:, c, part * HID + m * P:part * HID + m * P + n],
                                                 x_t[s][:, c, 1:1 + TOKENS], c == 0, c == FC - 1)) for c in range(FC)], n

                for m0 in range(0, HC, 2):
                    tile = wide.take()
                    for m in (m0, m0 + 1):
                        steps, n = up(1, m)
                        dst = tile.buf[0:n, (m - m0) * 512:(m - m0) * 512 + 512]
                        for one in steps:
                            last = pe.do(one(dst), [ready, weights["w_up"], tile.free], "up")
                        got = dve.do(lambda e, m=m, n=n, dst=dst: e.tensor_scalar(
                            gate[0:n, m, :], dst, bias_up[0:n, HC + m:HC + m + 1], None, ALU.add),
                            [last, o_read, weights["small"]], "gate")
                    wide.give(tile, got)
                    yield
                act.do(lambda e: e.activation(gate[:, 0:HC - 1, :], gate[:, 0:HC - 1, :], ACT.Gelu), got, "gelu")
                gated = act.do(lambda e: e.activation(gate[0:HLAST, HC - 1, :], gate[0:HLAST, HC - 1, :], ACT.Gelu),
                               got, "gelu")
                for m0 in range(0, HC, 2):
                    tile = wide.take()
                    for m in (m0, m0 + 1):
                        steps, n = up(0, m)
                        dst = tile.buf[0:n, (m - m0) * 512:(m - m0) * 512 + 512]
                        for one in steps:
                            last = pe.do(one(dst), [ready, tile.free], "up")
                        got = dve.do(lambda e, m=m, n=n, dst=dst: e.scalar_tensor_tensor(
                            out=hidden[0:n, m, :], in0=dst, scalar=bias_up[0:n, m:m + 1], in1=gate[0:n, m, :],
                            op0=ALU.add, op1=ALU.mult), [last, gated, blank], "hidden")
                    wide.give(tile, got)
                    yield
                finish("w_up", s, last)
                yield from claim("w_down", stage)
                tile = wide.take()
                for t in range(TILES):
                    for m in range(HC):
                        last = pe.do(mm(tile.buf[:, t * DIM:(t + 1) * DIM], hidden[:, m, t * P:(t + 1) * P],
                                        w_down[:, m, :], m == 0, m == HC - 1),
                                     [got, tile.free, weights["w_down"]], "down")
                finish("w_down", s, last)
                added = dve.do(lambda e: e.tensor_tensor(flat_resid, tile.buf[:, :], flat_resid, ALU.add),
                               [last, biased], "resid")
                wide.give(tile, added)
                finish("small", s, [added, ready])
                resid_done[b] = [added]
                stream_free[s] = [last, got]
                if is_last:
                    back = x_n[s][:, :, :].rearrange("p t f -> p (t f)")
                    loaded = load(back, d["saved"][b], [xn_free[s], saves[b]], f"back{s}")
                    yield
                    added = pool.do(lambda e: e.tensor_tensor(flat_resid, flat_resid, back, ALU.add),
                                    [loaded, added], "resid")
                    xn_free[s] = [added]
                    resid_done[b] = [added]
                yield

            def attention_a(s, b, stage):
                q_t = work[s][:, 0].rearrange("p (c n) -> p c n", c=PAIRS)
                v = work[s][:, 1].rearrange("p (t n) -> p t n", t=TILES)
                o_t = work[s][:, 2].rearrange("p (c n) -> p c n", c=PAIRS)
                k_p = kpad[s][:, :].rearrange("p (c j n) -> p c j n", c=PAIRS, j=2)
                wq = w_in[:, 0:2 * INNER].rearrange("p (c n) -> p c n", c=FC)
                wd = w_in[:, 1024:1024 + FC * RANK].rearrange("p (c n) -> p c n", c=FC)
                wk, wv = w_in[:, 1152:1664], w_in[:, 1664:2176]
                zero_pads(s, "pairs")
                yield from claim("w_in", stage)
                stats = norm_stats(s, lambda t: [resid[:, b, t, :]], [resid_done[b], stream_free[s]])
                yield
                for t in range(TILES):
                    done = normalised(s, t, x_n[s][:, t, :], resid[:, b, t, :], [stats, xn_free[s]])
                yield
                ready = to_features(s, lambda t: x_n[s][:, t, :], [done], False)
                xn_free[s] = ready
                yield
                for c0 in range(0, PAIRS, 2):
                    tile = wide.take()
                    for c in (c0, c0 + 1):
                        for k in range(FC):
                            last = pe.do(mm(tile.buf[:, (c - c0) * 512:(c - c0) * 512 + 512], wq[:, k, c * P:(c + 1) * P],
                                            x_t[s][:, k, 1:1 + TOKENS], k == 0, k == FC - 1),
                                         [ready, weights["w_in"], tile.free], "qkv")
                    got_q = act.do(lambda e, c0=c0, tile=tile: e.activation(
                        q_t[:, c0:c0 + 2, :].rearrange("p c n -> p (c n)"), tile.buf[:, :], ACT.Copy, scale=HD ** -0.5),
                        [last, stream_free[s]], "q_t")
                    wide.give(tile, got_q)
                latent = x_n[s][:, 0:2, :].rearrange("p a n -> p (a n)")
                tile = wide.take()
                for k in range(FC):
                    last = pe.do(mm(tile.buf[0:RANK, 0:512], wd[:, k, :], x_t[s][:, k, 1:1 + TOKENS], k == 0, k == FC - 1),
                                 [tile.free], "qkv")
                blank = dve.do(lambda e: e.memset(latent[RANK:P, :], 0.0), ready, "blank")
                got = act.do(lambda e: e.activation(latent[0:RANK, :], tile.buf[0:RANK, 0:512], ACT.Copy),
                             [last, ready], "latent")
                wide.give(tile, got)
                yield
                for c0 in range(0, PAIRS, 2):
                    tile = wide.take()
                    for c in (c0, c0 + 1):
                        last = pe.do(mm(tile.buf[:, (c - c0) * 512:(c - c0) * 512 + 512], wk[:, c * P:(c + 1) * P],
                                        latent, True, True), [got, blank, tile.free], "qkv")
                    for j in range(2):
                        r = slice(64 * j, 64 * j + 64)
                        got_k = dve.do(lambda e, c0=c0, j=j, r=r, tile=tile: e.tensor_copy(
                            k_p[r, c0:c0 + 2, j, :], tile.buf[r, :].rearrange("p (c n) -> p c n", c=2)),
                            [last, stream_free[s], kpad_zero[s]], "k_t")
                    wide.give(tile, got_k)
                    tile = wide.take()
                    for t in (c0, c0 + 1):
                        last = pe.do(mm(tile.buf[:, (t - c0) * 512:(t - c0) * 512 + 512], latent[:, t * P:(t + 1) * P],
                                        wv, True, True), [got, blank, tile.free], "qkv")
                    got_v = act.do(lambda e, c0=c0, tile=tile: e.activation(
                        v[:, c0:c0 + 2, :].rearrange("p c n -> p (c n)"), tile.buf[:, :], ACT.Copy),
                        [last, stream_free[s]], "v")
                    wide.give(tile, got_v)
                    yield
                xn_free[s] = [last]
                finish("w_in", s, last)
                ready = [got_q, got_k, got_v]
                yield from claim("w_up", stage)
                out_marks = []
                held = Ring([prob_own[s], spare(s)])
                held.slots[0].free, held.slots[1].free = prob_free[s], spare_free[s]

                def softmax(step):
                    h, half = step
                    c, j = h // 2, h % 2
                    tile, st, pr = wide.take(), small.take(), held.take()
                    for i in range(2):
                        t = 2 * half + i
                        last = pe.do(mm(tile.buf[:, i * 512:i * 512 + 512], q_t[:, c, t * P:(t + 1) * P],
                                        k_p[:, c, j, :], True, True), [ready, tile.free], "score")
                    low = dve.do(lambda e: e.tensor_reduce(
                        st.buf[:, 0:2], tile.buf[:, :].rearrange("p (t n) -> p t n", t=2), AX, ALU.max,
                        negate=True), [last, st.free], "max")
                    for i in range(2):
                        cut = slice(i * 512, i * 512 + 512)
                        done = act.do(lambda e: e.activation(
                            pr.buf[:, cut], tile.buf[:, cut], ACT.Exp, bias=st.buf[:, i:i + 1],
                            accum_out=st.buf[:, 2 + i:3 + i]), [low, pr.free], "exp")
                    wide.give(tile, done)
                    return step, pr, st, done

                def normalise(step, pr, st, done):
                    inv = dve.do(lambda e: e.reciprocal(st.buf[:, 4:6], st.buf[:, 2:4]), done, "inv")
                    marks = []
                    for i, queue in ((0, pool), (1, dve)):
                        cut = slice(i * 512, i * 512 + 512)
                        marks.append(queue.do(lambda e: e.tensor_scalar(
                            pr.buf[:, cut], pr.buf[:, cut], st.buf[:, 4 + i:5 + i], 1.0,
                            ALU.mult, ALU.mult), [inv, done], "weight"))
                    small.give(st, marks)
                    return step, pr, marks

                def turn(step, pr, scaled):
                    tile, pt = wide.take(), prob_t[s].take()
                    for kb in range(TILES):
                        for i in range(2):
                            last = pe.do(tr(tile.buf[:, kb * 256 + i * P:kb * 256 + (i + 1) * P],
                                            pr.buf[:, i * 512 + kb * P:i * 512 + (kb + 1) * P]),
                                         [scaled, tile.free], "turn")
                    held.give(pr, last)
                    got1 = act.do(lambda e: e.activation(pt.buf[:, 0:512], tile.buf[:, 0:512], ACT.Copy),
                                  [last, pt.free], "prob_t")
                    got2 = dve.do(lambda e: e.tensor_copy(pt.buf[:, 512:1024], tile.buf[:, 512:1024]),
                                  [last, pt.free], "prob_t")
                    wide.give(tile, got1, got2)
                    return step, pt, [got1, got2]

                def mix(step, pt, turned):
                    h, half = step
                    c, j = h // 2, h % 2
                    if j == half == 0:
                        o_tiles.append(narrow[s].take())
                    o_tile = o_tiles[-1]
                    for kb in range(TILES):
                        last = pe.do(mm(o_tile.buf[64 * j:64 * j + 64, 256 * half:256 * half + 256],
                                        v[:, kb, h * HD:(h + 1) * HD], pt.buf[:, kb * 256:kb * 256 + 256],
                                        kb == 0 and half == 0, kb == TILES - 1),
                                     [turned, o_tile.free], "mix")
                    prob_t[s].give(pt, last)
                    if j == 1 and half == 1:
                        done = act.do(lambda e: e.activation(o_t[:, c, :], o_tile.buf[:, :], ACT.Copy),
                                      [last, stream_free[s]], "o_t")
                        narrow[s].give(o_tile, done)
                        out_marks.append(done)

                o_tiles = []
                yield from in_turns([(h, half) for h in range(HEADS) for half in range(2)],
                                    softmax, normalise, turn, mix)
                prob_free[s], spare_free[s] = held.slots[0].free, held.slots[1].free
                finish("w_up", s, spare_free[s])
                yield from claim("w_out", stage)
                o_read, added = project_out(s, b, lambda c: o_t[:, c, :], PAIRS, out_marks)
                resid_done[b] = [added]
                stream_free[s] = [o_read]
                yield

            def attention_causal(s, b, stage):
                q_a = work[s][:, 0].rearrange("p (g t n) -> p g t n", g=GROUPS, t=TILES)
                k_a = work[s][:, 1].rearrange("p (g t n) -> p g t n", g=GROUPS, t=TILES)
                v = work[s][:, 2].rearrange("p (t n) -> p t n", t=TILES)
                q_rows, qd_rows = (x_t[s][:, i, 1:1 + TOKENS] for i in range(2))
                k_rows = x_n[s][:, 2:4, :].rearrange("p t f -> p (t f)")
                k_p = kpad[s][:, :].rearrange("p (o h n) -> p o h n", o=2, h=4)
                w = w_in[:, 0:FC * 3 * DIM].rearrange("p (c n) -> p c n", c=FC)
                zero_pads(s, "fours")
                yield from claim("w_in", stage)
                yield from claim("small", stage)
                yield from claim("w_up", stage)
                stats = norm_stats(s, lambda t: [resid[:, b, t, :]], [resid_done[b], stream_free[s]])
                yield
                for t in range(TILES):
                    done = normalised(s, t, x_n[s][:, t, :], resid[:, b, t, :], [stats, xn_free[s]])
                biased = pool.do(lambda e: e.tensor_tensor(
                    resid[:, b], resid[:, b], bias_row[:, :].unsqueeze(1).to_broadcast([P, TILES, DIM]), ALU.add),
                    [done, resid_done[b], weights["small"]], "bias")
                resid_done[b] = [biased]
                blank = [pool.do(lambda e, i=i: e.memset(work[s][:, i, :], 0.0), stream_free[s], "blank") for i in range(3)]
                rows4 = lambda a: a.rearrange("p g t (h e) -> p (g t) h e", e=BROW)
                pool.do(lambda e: e.memset(rows4(q_a)[:, :, :, BHD + 1:BHD + 2], 1.0), blank, "blank")
                blank = pool.do(lambda e: e.memset(rows4(k_a)[:, :, :, BHD:BHD + 1], 1.0), blank, "blank")
                yield
                ready = to_features(s, lambda t: x_n[s][:, t, :], [done], False)
                xn_free[s] = ready
                yield
                ends = []
                for t in range(TILES):
                    tile = wide.take()
                    for c in range(FC):
                        for lo, n in ((0, 512), (512, 256)):
                            last = pe.do(mm(tile.buf[:, lo:lo + n], x_t[s][:, c, 1 + t * P:1 + (t + 1) * P],
                                            w[:, c, lo:lo + n], c == 0, c == FC - 1),
                                         [ready, weights["w_in"], tile.free], "qkv")
                    row = Slot(spare(s))
                    got = dve.do(lambda e, tile=tile, row=row: e.tensor_tensor(
                        row.buf[:, 0:3 * DIM], tile.buf[:, 0:3 * DIM], qkv_bias, ALU.add),
                        [last, spare_free[s], weights["small"]], "raw")
                    wide.give(tile, got)
                    sq, ss, sk = prob_own[s], small.take(), small.take()
                    squared = act.do(lambda e, row=row, sq=sq: e.activation(
                        sq[:, 0:2 * DIM], row.buf[:, 0:2 * DIM], ACT.Square), [got, prob_free[s]], "square")
                    for z, one in ((0, ss), (1, sk)):
                        summed = dve.do(lambda e, z=z, one=one, sq=sq: e.tensor_reduce(
                            one.buf[:, 0:16], sq[:, z * DIM:(z + 1) * DIM].rearrange("p (h e) -> p h e", e=BHD),
                            AX, ALU.add), [squared, one.free], "ss")
                    prob_free[s] = [summed]
                    head = lambda a: a.rearrange("p (g h e) -> p g h e", g=GROUPS, e=BHD)
                    slot = lambda a, t, lo, n: a[:, :, t, :].rearrange("p g (h e) -> p g h e", e=BROW)[:, :, :, lo:lo + n]
                    one4 = lambda a: a[:, 0:16].rearrange("p (g h e) -> p g h e", g=GROUPS, e=1)
                    w1 = pool.do(lambda e, t=t, row=row: e.tensor_scalar(slot(q_a, t, 0, BHD), head(row.buf[:, 0:DIM]),
                                                                         -2.0, 1.0, ALU.mult, ALU.mult), [got, blank], "rows")
                    w2 = pool.do(lambda e, t=t, row=row: e.tensor_scalar(slot(k_a, t, 0, BHD), head(row.buf[:, DIM:2 * DIM]),
                                                                         1.0, 1.0, ALU.mult, ALU.mult), [got, blank], "rows")
                    w3 = pool.do(lambda e, t=t, ss=ss: e.tensor_scalar(slot(q_a, t, BHD, 1), one4(ss.buf), EPS_B, 1.0,
                                                                       ALU.add, ALU.mult), [summed, blank], "rows")
                    w4 = pool.do(lambda e, t=t, sk=sk: e.tensor_scalar(slot(k_a, t, BHD + 1, 1), one4(sk.buf), 1.0, 1.0,
                                                                       ALU.mult, ALU.mult), [summed, blank], "rows")
                    w5 = act.do(lambda e, t=t, row=row: e.activation(
                        v[:, t, :].rearrange("p (h e) -> p h e", e=BROW)[:, :, 0:BHD],
                        row.buf[:, 2 * DIM:3 * DIM].rearrange("p (h e) -> p h e", e=BHD), ACT.Copy), [got, blank], "v")
                    spare_free[s] = [squared, w4, w5]
                    small.give(ss, w4)
                    small.give(sk, w4)
                    ends = [w4, w5]
                    yield
                qkv_read = last
                finish("w_in", s, [last, got])
                finish("small", s, biased)
                out_marks = []
                held = Ring([prob_own[s], spare(s)])
                held.slots[0].free, held.slots[1].free = prob_free[s], spare_free[s]
                o_tiles, rows_done = [], []
                inverse = Ring([x_n[s][:, 0:2, :].rearrange("p t f -> p (t f)")])
                inverse.slots[0].free = xn_free[s]
                inverse.slots.append(scratch[s])

                def group_rows(g):
                    tile = wide.take()
                    for t in range(TILES):
                        pe.do(tr(tile.buf[:, t * P:(t + 1) * P], q_a[:, g, t, :]), [ends, tile.free], "turn")
                        last = pe.do(tr(tile.buf[:, 512 + t * P:512 + (t + 1) * P], k_a[:, g, t, :]), [ends], "turn")
                    a1 = act.do(lambda e: e.activation(q_rows, tile.buf[:, 0:512], ACT.Copy),
                                [last, group_free[s], qkv_read], "q_t")
                    a2 = act.do(lambda e: e.activation(k_rows, tile.buf[:, 512:1024], ACT.Copy),
                                [last, spread_last[s], ready], "k_t")
                    a3 = dve.do(lambda e: e.tensor_scalar(qd_rows, tile.buf[:, 0:512], dot_rows[:, 0:1], None,
                                                          ALU.mult), [a1, group_free[s], qkv_read, consts], "q_t")
                    wide.give(tile, a1, a2, a3)
                    o = g % 2
                    for j in range(4):
                        spread = load(k_p[32 * j:32 * j + 32, o, j, :], k_rows[32 * j:32 * j + 32, :],
                                      [a2, kpad_zero[s], pad_free[s][o]], f"spread{s}")
                    spread_last[s] = [spread]
                    rows_done[:] = [a1, a3, spread]
                    return True

                def softmax(step):
                    g, j, half = step
                    o = g % 2
                    st, pr = small.take(), held.take()
                    for i in range(2):
                        t = 2 * half + i
                        n = P * (t + 1)
                        tile = wide.take()
                        pe.do(mm(tile.buf[:, 0:n], qd_rows[:, t * P:(t + 1) * P], k_p[:, o, j, 0:n], True, True),
                              [rows_done, tile.free], "score")
                        last = pe.do(mm(tile.buf[:, 512:512 + n], q_rows[:, t * P:(t + 1) * P], k_p[:, o, j, 0:n],
                                        True, True), [rows_done], "score")
                        group_free[s] = pad_free[s][o] = [last]
                        cut, own = slice(i * 512, i * 512 + n), slice(i * 512 + n - P, i * 512 + n)
                        inv_t = inverse.take()
                        den = dve.do(lambda e: e.reciprocal(inv_t.buf[:, 0:n], tile.buf[:, 512:512 + n]),
                                     [last, inv_t.free], "inv")
                        num = act.do(lambda e: e.activation(pr.buf[:, cut], tile.buf[:, 0:n], ACT.Square, scale=0.5),
                                     [last, pr.free], "square")
                        wide.give(tile, num, den)
                        high = st.free
                        if t:
                            early = slice(i * 512, i * 512 + n - P)
                            high = dve.do(lambda e: e.tensor_tensor_reduce(
                                pr.buf[:, early], pr.buf[:, early], inv_t.buf[:, 0:n - P], 1.0, -LOW,
                                ALU.mult, ALU.max, st.buf[:, 8 + i:9 + i]), [num, den, st.free], "max")
                        ratio = dve.do(lambda e: e.tensor_tensor(
                            pr.buf[:, own], pr.buf[:, own], inv_t.buf[:, n - P:n], ALU.mult), [num, den], "ratio")
                        inverse.give(inv_t, ratio)
                        low = dve.do(lambda e: e.tensor_tensor_reduce(
                            pr.buf[:, own], pr.buf[:, own], causal_mask[:, 0:P], 1.0,
                            st.buf[:, 8 + i:9 + i] if t else -LOW, ALU.add, ALU.max, st.buf[:, i:i + 1]),
                            [ratio, high, consts], "max")
                    low = dve.do(lambda e: e.tensor_scalar(st.buf[:, 2:4], st.buf[:, 0:2], -1.0, None, ALU.mult),
                                 low, "max")
                    for i in range(2):
                        n = P * (2 * half + i + 1)
                        done = act.do(lambda e: e.activation(
                            pr.buf[:, i * 512:i * 512 + n], pr.buf[:, i * 512:i * 512 + n], ACT.Exp,
                            bias=st.buf[:, 2 + i:3 + i], accum_out=st.buf[:, 4 + i:5 + i]), low, "exp")
                    return step, pr, st, done

                def normalise(step, pr, st, done):
                    g, j, half = step
                    inv = dve.do(lambda e: e.reciprocal(st.buf[:, 6:8], st.buf[:, 4:6]), done, "inv")
                    for i in range(2):
                        n = P * (2 * half + i + 1)
                        scaled = pool.do(lambda e: e.tensor_scalar(
                            pr.buf[:, i * 512:i * 512 + n], pr.buf[:, i * 512:i * 512 + n], st.buf[:, 6 + i:7 + i],
                            1.0, ALU.mult, ALU.mult), [inv, done], "weight")
                    small.give(st, scaled)
                    return step, pr, scaled

                def turn(step, pr, scaled):
                    g, j, half = step
                    tile, pt = wide.take(), prob_t[s].take()
                    blocks = [(kb, i) for kb in range(2 * half + 2) for i in range(2) if kb <= 2 * half + i]
                    for kb, i in blocks:
                        last = pe.do(tr(tile.buf[:, kb * 256 + i * P:kb * 256 + (i + 1) * P],
                                        pr.buf[:, i * 512 + kb * P:i * 512 + (kb + 1) * P]),
                                     [scaled, tile.free], "turn")
                    held.give(pr, last)
                    got = []
                    for bank in range(half + 1):
                        pieces = [(512 * bank, 512)] if bank < half else [(512 * bank, 256), (512 * bank + 384, P)]
                        for at, w_ in pieces:
                            got = act.do(lambda e: e.activation(pt.buf[:, at:at + w_], tile.buf[:, at:at + w_],
                                                                ACT.Copy), [last, pt.free], "prob_t")
                    wide.give(tile, got)
                    return step, pt, got

                def mix(step, pt, turned):
                    g, j, half = step
                    h = 4 * g + j
                    if j == half == 0:
                        o_tiles.append(narrow[s].take())
                    o_tile = o_tiles[-1]
                    for kb in range(2 * half + 2):
                        i = 1 if kb == 2 * half + 1 else 0
                        last = pe.do(mm(o_tile.buf[32 * j:32 * j + 32, 256 * half + i * P:256 * half + 256],
                                        v[:, kb, h * BROW:(h + 1) * BROW],
                                        pt.buf[:, kb * 256 + i * P:kb * 256 + 256],
                                        kb == 0 and half == 0, kb == 2 * half + 1), [turned, o_tile.free], "mix")
                    prob_t[s].give(pt, last)
                    if j == 3 and half == 1:
                        out = q_a[:, g].rearrange("p t n -> p (t n)")
                        done = act.do(lambda e: e.activation(out, o_tile.buf[:, :], ACT.Copy), last, "o_t")
                        narrow[s].give(o_tile, done)
                        out_marks.append(done)

                yield from in_turns([(g, j, half) for g in range(GROUPS) for j in range(4) for half in range(2)],
                                    softmax, normalise, turn, mix,
                                    lambda step: group_rows(step[0]) if step[1:] == (0, 0) else None)
                prob_free[s], spare_free[s] = held.slots[0].free, held.slots[1].free
                xn_free[s] = [inverse.slots[0].free, spread_last[s]]
                finish("w_up", s, spare_free[s])
                yield from claim("w_out", stage)
                o_read, added = project_out(s, b, lambda c: q_a[:, c].rearrange("p t n -> p (t n)"), GROUPS, out_marks)
                resid_done[b] = [added]
                stream_free[s] = [o_read]
                yield

            rows_free = {"raw": [], "sin": []}
            prob_free, spare_free, spread_last = ([[], []] for _ in range(3))
            shift_free, xn_free, group_free = [[], []], [[], []], [[], []]
            pad_free = [[[], []], [[], []]]
            saves = {}
            kpad_zero = [[], []]
            qkv_bias = w_in[:, 2304:2304 + 3 * DIM]

            def load_weights(name, stage, depth):
                free = flat(list(weight_users[name].values()))
                over = lambda a, c: a.rearrange("p (c n) -> p c n", c=c)
                rows_of = lambda a: a.rearrange("(c p) n -> p c n", p=P)
                if name == "w_up" and stage != "f":
                    for s in range(2):
                        spare_free[s] = free
                elif name == "w_in" and stage == "a":
                    pads = dve.do(lambda e: e.memset(w_in[RANK:P, 1152:2176], 0.0), free, "wpad")
                    load(over(w_in[:, 0:1024], FC), rows_of(d["a_wq_t"]), free, name)
                    load(over(w_in[:, 1024:1152], FC), rows_of(d["a_wd_t"]), free, name)
                    load(w_in[0:RANK, 1152:1664], d["a_wk_t"], free, name)
                    weights[name] = [load(w_in[0:RANK, 1664:2176], d["a_wv_t"], free, name), pads]
                elif name == "w_out" and stage == "a":
                    weights[name] = [load(over(w_out[:, :], PAIRS), rows_of(d["a_wo_t"]), free, name)]
                elif name == "w_in" and stage == "b":
                    load(over(w_in[:, 0:FC * 3 * DIM], FC), rows_of(d["b_wqkv"]), free, name)
                    weights[name] = [load(qkv_bias, d["b_bqkv"].unsqueeze(0).to_broadcast([P, 3 * DIM]), free, name)]
                elif name == "w_out" and stage == "b":
                    zero = pool.do(lambda e: e.memset(w_out[:, :], 0.0), free, "wpad")
                    for j in range(4):
                        last = load(over(w_out[32 * j:32 * j + BHD, :], GROUPS),
                                    d["b_wout"].rearrange("(g j e) n -> j e g n", g=GROUPS, e=BHD)[j], zero, name)
                    weights[name] = [last]
                elif name == "small" and stage == "b":
                    weights[name] = [load(bias_row[:, :], d["b_bout"].unsqueeze(0).to_broadcast([P, DIM]), free, name),
                                     weights["w_in"]]
                elif name == "w_in":
                    weights[name] = [load(over(w_in[:, :], FC), rows_of(d["f_wqkv"][depth]), free, name)]
                elif name == "w_out":
                    weights[name] = [load(over(w_out[:, :], PAIRS), rows_of(d["f_wo"][depth]), free, name)]
                elif name == "w_up":
                    weights[name] = [load(w_up[:, :, :], rows_of(d["f_w1"][depth]), free, name)]
                elif name == "w_down":
                    zero = pool.do(lambda e: e.memset(w_down[:, HC - 1, :], 0.0), free, "wpad")
                    load(w_down[:, 0:HC - 1, :], rows_of(d["f_w2"][depth, 0:(HC - 1) * P]), free, name)
                    weights[name] = [load(w_down[0:HLAST, HC - 1, :], d["f_w2"][depth, (HC - 1) * P:HID], zero, name)]
                else:
                    load(rot[:, :, :, :], d["rotary"], free, name)
                    load(qk_scale[:, 0, :], d["f_qs"][depth].unsqueeze(0).to_broadcast([P, HD]), free, name)
                    load(qk_scale[:, 1, :], d["f_ks"][depth].unsqueeze(0).to_broadcast([P, HD]), free, name)
                    load(ln_gb[:, 0, :], d["f_lg"][depth].rearrange("(c p) -> p c", p=P), free, name)
                    load(ln_gb[:, 1, :], d["f_lb"][depth].rearrange("(c p) -> p c", p=P), free, name)
                    for part in range(2):
                        lo = part * HID
                        load(bias_up[:, part * HC:part * HC + HC - 1],
                             d["f_b1"][depth, lo:lo + (HC - 1) * P].rearrange("(c p) -> p c", p=P), free, name)
                        load(bias_up[0:HLAST, part * HC + HC - 1:part * HC + HC],
                             d["f_b1"][depth, lo + (HC - 1) * P:lo + HID].unsqueeze(1), free, name)
                    last = load(bias_row[:, :], d["f_b2"][depth].unsqueeze(0).to_broadcast([P, DIM]), free, name)
                    for z in range(2):
                        whole = qk_scale[:, z, :].unsqueeze(1).to_broadcast([P, TILES, HD])
                        swap = qk_scale[:, z, :].rearrange("p (u e) -> p u e", u=2)[:, ::-1, :].unsqueeze(1)\
                            .to_broadcast([P, TILES, 2, HD // 2])
                        pool.do(lambda e: e.tensor_tensor(rot[:, 2 * z], rot[:, 2 * z], whole, ALU.mult), last, "tables")
                        table = rot[:, 2 * z + 1].rearrange("p t (u e) -> p t u e", u=2)
                        made = pool.do(lambda e: e.tensor_tensor(table, table, swap, ALU.mult), last, "tables")
                    weights[name] = [made, last]

            holds, pending = {}, {}

            def claim(name, n):
                while holds.get(name) != n:
                    if pending.get(name, 0):
                        yield
                    else:
                        load_weights(name, *PLAN[n])
                        holds[name], pending[name] = n, SEQS

            def finish(name, s, marks):
                weight_users[name][s] = flat(marks)
                pending[name] -= 1

            def spare(s):
                return w_up[:, :, :].rearrange("p c n -> p (c n)")[:, s * 1024:(s + 1) * 1024]

            pad_kind = [None, None]

            def zero_pads(s, kind):
                if pad_kind[s] != kind:
                    pad_kind[s] = kind
                    kpad_zero[s] = [pool.do(lambda e: e.memset(kpad[s][:, :], 0.0),
                                            [stream_free[s], pad_free[s]], "kpad")]

            def unit(n, b):
                stage, depth = PLAN[n]
                if stage == "a":
                    return lambda s: attention_a(s, b, n)
                if stage == "b":
                    return lambda s: attention_causal(s, b, n)
                return lambda s: local_layer(s, b, n, depth == 0, depth == DEPTH - 1)

            waiting = [unit(n, b) for n in range(len(PLAN)) for b in range(SEQS)]
            flying, places, rounds = [], [0, 1], 0
            while waiting or flying:
                while waiting and places and (places[0] == 0 or rounds >= STAGGER):
                    s = places.pop(0)
                    flying.append((s, waiting.pop(0)(s)))
                rounds += 1
                for item in list(flying):
                    if next(item[1], "end") == "end":
                        flying.remove(item)
                        places.append(item[0])
            stored = [sp.do(lambda e, b=b: e.dma_start(d["out"][b].rearrange("(t p) f -> p t f", p=P), resid[:, b]),
                            resid_done[b], "out", 16) for b in range(SEQS)]
            sp.wait(stored[-1])

        block = stack.enter_context(nc.Block())
        for live in ("tensor", "scalar", "vector", "gpsimd", "sync"):
            engine_block = {"tensor": block.tensor, "scalar": block.scalar, "vector": block.vector,
                            "gpsimd": block.gpsimd, "sync": block.sync}[live]
            engine_block(lambda eng, live=live: schedule(live, eng))


STAGGER = 20
PLAN = [("a", 0), ("f", 0), ("f", 1), ("b", 0), ("f", 0), ("f", 1)]


def constants():
    half = np.arange(0, HD, 2, dtype=np.float32)
    inv_freq = (1.0 / np.float32(10000.0) ** (half / np.float32(HD))).astype(np.float32)
    t = np.arange(TOKENS, dtype=np.float32)
    freqs = (t[:, None] * inv_freq[None, :]).astype(np.float32)
    freqs = np.concatenate([freqs, freqs], axis=-1)
    base = (half + 0.4 * HD) / (1.4 * HD)
    power = (t - TOKENS // 2) / float(WINDOW // 2)
    scale = base[None, :].astype(np.float64) ** power[:, None].astype(np.float64)
    scale = np.concatenate([scale, scale], axis=-1)
    cos, sin = np.cos(freqs.astype(np.float64)), np.sin(freqs.astype(np.float64))
    sign = np.where(np.arange(HD) < HD // 2, -1.0, 1.0)
    tables = [8.0 * cos * scale, 8.0 * sin * sign * scale, cos / scale, sin * sign / scale]
    rotary = np.stack([x.reshape(TILES, P, HD) for x in tables]).transpose(2, 0, 1, 3)
    i, j = np.arange(P)[:, None], np.arange(P)[None, :]
    own = np.where(j > i, MASKED, 0.0)
    previous = np.where(j < i, MASKED, 0.0)
    return {
        "ident": np.eye(P), "rotary": rotary,
        "local_mask": np.concatenate([previous, own], axis=1),
        "causal_mask": own,
        "dot_rows": (np.arange(P)[:, None] % BROW < BHD) * 1.0,
    }


WINDOW = 128


def kernel(**inputs):
    import concourse.bacc as bacc
    from concourse.bass_utils import run_bass_kernel_spmd

    given = {k: np.asarray(v) for k, v in inputs.items()}
    a, bb, f = "L0_attn_a_", "L0_attn_b_", "L0_ffn_"
    arrays = {
        "x": given[a + "x"], "a_wq_t": given[a + "Wq"].T, "a_wd_t": given[a + "Wkv_down"].T,
        "a_wk_t": given[a + "Wk_up"].T, "a_wv_t": given[a + "Wv_up"].T, "a_wo_t": given[a + "Wo"].T,
        "b_wqkv": given[bb + "w_qkv"], "b_bqkv": given[bb + "b_qkv"], "b_wout": given[bb + "w_out"],
        "b_bout": given[bb + "b_out"], "f_wqkv": given[f + "wqkv"], "f_qs": given[f + "q_scale"],
        "f_ks": given[f + "k_scale"], "f_wo": given[f + "wo"], "f_lg": given[f + "ln_g"], "f_lb": given[f + "ln_b"],
        "f_w1": given[f + "w1"], "f_b1": given[f + "b1"], "f_w2": given[f + "w2"], "f_b2": given[f + "b2"],
    }
    arrays.update({k: v.astype(np.float32) for k, v in constants().items()})
    arrays = {"in_" + k: np.ascontiguousarray(v) for k, v in arrays.items()}
    nc = bacc.Bacc("TRN2", target_bir_lowering=False, num_devices=1)
    d = {k[3:]: nc.dram_tensor(k, v.shape, F32, kind="ExternalInput").ap() for k, v in arrays.items()}
    d["out"] = nc.dram_tensor("out", (SEQS, TOKENS, DIM), F32, kind="ExternalOutput").ap()
    d["saved"] = nc.dram_tensor("saved", (SEQS, P, TILES * DIM), F32).ap()
    build(nc, d)
    result = run_bass_kernel_spmd(nc, [arrays], core_ids=[0])
    return result.results[0]["out"]
```

```python
from contextlib import ExitStack

import numpy as np

import concourse.bass as bass
from concourse import mybir

F32 = mybir.dt.float32
ALU = mybir.AluOpType
ACT = mybir.ActivationFunctionType
AX = mybir.AxisListType.X

P = 128
SEQS, TOKENS, DIM = 8, 512, 256
TILES = TOKENS // P
FC = DIM // P
HEADS, HD = 8, 64
INNER = HEADS * HD
PAIRS = HEADS // 2
RANK = 64
BHEADS, BHD, BROW = 16, 16, 32
GROUPS = BHEADS * BROW // P
HID = int(DIM * 4 * 2 / 3)
HC = -(-HID // P)
HLAST = HID - (HC - 1) * P
DEPTH = 2
FEW = 3 * P
EPS_LN, EPS_B = 1e-5, 1e-6
DEN_MIN, DEN_MAX = 1e-12, 2.0 ** 62
MASKED = -1e30
LOW = 3e38
EXP_TABLES = "natural_log_exp_and_others"
GELU_TABLES = "gelu"


class Mark:

    def __init__(self, sem, value):
        self.sem, self.value, self.at = sem, value, 0.0


class Signals:

    def __init__(self, nc, stack):
        self.nc, self.stack, self.sems, self.counts = nc, stack, {}, {}

    def restart(self):
        self.counts = {}

    def count(self, name, step):
        if name not in self.sems:
            self.sems[name] = self.stack.enter_context(self.nc.semaphore("s_" + name))
        self.counts[name] = self.counts.get(name, 0) + step
        return Mark(self.sems[name], self.counts[name])


class Queue:

    def __init__(self, name, signals, eng):
        self.name, self.signals, self.eng, self.seen, self.clock = name, signals, eng, {}, 0.0

    def do(self, emit, waits=(), signal="done", step=1):
        mark = self.signals.count(f"{self.name}_{signal}", step)
        start, kind = max(self.clock, when(waits) + 0.1), signal.rstrip("0123456789")
        mark.at = start + COSTS.get((self.name, kind), 0.3)
        self.clock = start + 0.3 if self.name == "sp" else mark.at
        if self.eng is not None:
            self.wait(waits)
            emit(self.eng).then_inc(mark.sem, step)
        return mark

    def wait(self, waits):
        if self.eng is None:
            return
        for mark in flat(waits):
            if self.seen.get(id(mark.sem), 0) < mark.value:
                self.seen[id(mark.sem)] = mark.value
                self.eng.wait_ge(mark.sem, mark.value)


def flat(waits):
    if isinstance(waits, Mark):
        return [waits]
    return [m for w in waits for m in flat(w)]


BLOCKED = Mark(None, 0)
BLOCKED.at = float("inf")


def when(marks):
    return max((m.at for m in flat(marks)), default=0.0)


class Slot:

    def __init__(self, buf):
        self.buf, self.free, self.taken = buf, [], False


class Ring:

    def __init__(self, bufs):
        self.slots, self.next = [Slot(b) for b in bufs], 0

    def take(self):
        slot = self.slots[self.next % len(self.slots)]
        assert not slot.taken, "a ring's buffer is still in use"
        slot.taken = True
        self.next += 1
        return slot

    def when(self):
        return self.slots[self.next % len(self.slots)].free

    @staticmethod
    def give(slot, *marks):
        slot.free, slot.taken = list(marks), False


def build(nc, d):
    stack = ExitStack()
    with stack:
        sig = Signals(nc, stack)
        def sb(name, *shape):
            return stack.enter_context(nc.sbuf_tensor(name, [P, *shape], F32))

        resid = sb("resid", SEQS, TILES, DIM)
        w_in = sb("w_in", 3072)
        w_out = sb("w_out", 1024)
        w_up = sb("w_up", FC, 2 * HID)
        w_down = sb("w_down", HC, DIM)
        rot = sb("rot", 4, TILES, HD)
        qk_scale = sb("qk_scale", 2, HD)
        ln_gb = sb("ln_gb", 2, FC)
        bias_up = sb("bias_up", 2 * HC)
        bias_row = sb("bias_row", DIM)
        ident = sb("ident", P)
        local_mask = sb("local_mask", 2 * P)
        causal_mask = sb("causal_mask", P)
        minus_half = sb("minus_half", 64)
        dot_rows = sb("dot_rows", 1)
        work = [sb(f"work{s}", 3, 4 * TOKENS) for s in range(2)]
        kpad = [sb(f"kpad{s}", 8 * TOKENS) for s in range(2)]
        x_t = [sb(f"x_t{s}", FC, TOKENS + 1) for s in range(2)]
        x_n = [sb(f"x_n{s}", TILES, DIM) for s in range(2)]
        shifted = [sb(f"shifted{s}", TILES, P) for s in range(2)]
        stat = [sb(f"stat{s}", 256) for s in range(2)]
        w_down_flat = w_down[:, :, :].rearrange("p c n -> p (c n)")
        rot_flat = rot[:, :, :, :].rearrange("p a t n -> p (a t n)")
        rows = sb("rows", 2, 2 * TOKENS)
        scratch_buf = sb("scratch", 2 * TOKENS)
        prob_own = [sb(f"prob{s}", 2 * TOKENS) for s in range(2)]
        prob_t_bufs = [sb(f"prob_t{i}", 2 * TOKENS) for i in range(2)]
        small_bufs = [sb(f"small{i}", 16) for i in range(16)]

        wide_bufs = [stack.enter_context(nc.psum_tensor(f"wide{i}", [P, 1024], F32)) for i in range(3)]
        narrow_bufs = [stack.enter_context(nc.psum_tensor(f"narrow{i}", [P, 512], F32)) for i in range(2)]

        def schedule(live, eng):
            sig.restart()
            pe, act, dve, pool, sp = (Queue(n, sig, eng if n2 == live else None) for n, n2 in (
                ("pe", "tensor"), ("act", "scalar"), ("dve", "vector"), ("pool", "gpsimd"), ("sp", "sync")))
            small = Ring(small_bufs)
            scratch = [Slot(scratch_buf[:, 0:512]), Slot(scratch_buf[:, 512:1024])]
            prob_t = [Ring([buf]) for buf in prob_t_bufs]
            wide = Ring(wide_bufs)
            narrow = [Ring([buf]) for buf in narrow_bufs]
            def load(dst, src, waits, signal):
                return sp.do(lambda e: e.dma_start(dst, src, allow_slow_non_contiguous=True), waits, signal, 16)

            consts = [
                load(ident[:, :], d["ident"], [], "const"),
                load(local_mask[:, :], d["local_mask"], [], "const"),
                load(causal_mask[:, :], d["causal_mask"], [], "const"),
                load(dot_rows[:, :], d["dot_rows"], [], "const"),
            ][-1]
            consts = [consts, pool.do(lambda e: e.memset(minus_half[:, :], -0.5), [], "zero")]
            arrived = [load(resid[:, b], d["x"][b].rearrange("(t p) f -> p t f", p=P), [], f"x{b}")
                       for b in range(SEQS)]
            resid_done = [[m] for m in arrived]
            for s in range(2):
                first = pool.do(lambda e, s=s: e.memset(x_t[s][:, :, 0:1], 0.0), [], "zero")
                first = pool.do(lambda e, s=s: e.memset(shifted[s][:, :, :], 0.0), [], "zero")
                consts.append(first)

            weights = {}
            weight_users = {k: {} for k in ("w_in", "w_out", "w_up", "w_down", "small")}
            stream_free = [[], []]

            table = [None]

            def tables(name):
                if table[0] != name:
                    table[0] = name
                    if act.eng is not None and name is not GELU_TABLES:
                        act.eng.preload_act_table_set(name)

            def mm(out, lhsT, rhs, start, stop, **k):
                return lambda e: e.matmul(out, lhsT, rhs, start=start, stop=stop, skip_group_check=True, **k)

            def tr(out, in_):
                return lambda e: e.transpose(out, in_, ident[0:in_.shape[0], 0:in_.shape[0]])

            def norm_stats(s, pieces, waits):
                st = stat[s]
                n = len(pieces(0))
                for i in range(n):
                    if i:
                        yield waits[i]
                    for t in range(TILES):
                        got = dve.do(lambda e: e.bn_stats(
                            st[:, (t * 2 + i) * 6:(t * 2 + i) * 6 + 6], pieces(t)[i]), waits[i], "stat")
                for t in range(TILES):
                    got = dve.do(lambda e, t=t: e.bn_aggr(
                        st[:, 64 + 2 * t:66 + 2 * t], st[:, t * 12:t * 12 + 6 * n]), got, "stat")
                var = st[:, 64:64 + 2 * TILES].rearrange("p (t c) -> p t c", c=2)[:, :, 1]
                eps = dve.do(lambda e: e.tensor_scalar(st[:, 80:80 + TILES], var, EPS_LN, None, ALU.add), got, "stat")
                power = pool.do(lambda e: e.tensor_tensor(st[:, 96:96 + TILES], st[:, 80:80 + TILES],
                                                          minus_half[:, 0:TILES], ALU.pow), [eps, consts], "rstd")
                return [got, power]

            def normalised(s, t, dst, src, waits):
                st = stat[s]
                return dve.do(lambda e: e.tensor_scalar(dst, src, st[:, 64 + 2 * t:65 + 2 * t],
                                                        st[:, 96 + t:97 + t], ALU.subtract, ALU.mult), waits, "norm")

            def to_features(s, src, waits, shift, scaled=None):
                done = []
                tile = wide.take()
                for c in range(FC):
                    for t in range(TILES):
                        last = pe.do(tr(tile.buf[:, c * TOKENS + t * P:c * TOKENS + (t + 1) * P],
                                        src(t)[:, c * P:(c + 1) * P]), [waits, tile.free, consts], "turn")
                for c in range(FC):
                    dst = x_t[s][:, c, 1:1 + TOKENS]
                    ps = tile.buf[:, c * TOKENS:(c + 1) * TOKENS]
                    if scaled is None:
                        done.append(act.do(lambda e, dst=dst, ps=ps: e.activation(dst, ps, ACT.Copy),
                                           [last, stream_free[s]], "x_t"))
                    else:
                        done.append(dve.do(lambda e, dst=dst, ps=ps, c=c: e.tensor_scalar(
                            dst, ps, ln_gb[:, 0, c:c + 1], ln_gb[:, 1, c:c + 1], ALU.mult, ALU.add),
                            [last, stream_free[s], scaled], "x_t"))
                wide.give(tile, done)
                return done

            def project_out(s, b, out_t, chunks, rows_done, extra=None):
                tile = wide.take()
                for t in range(TILES):
                    for c in range(chunks):
                        last = pe.do(mm(tile.buf[:, t * DIM:(t + 1) * DIM], out_t(c)[:, t * P:(t + 1) * P],
                                        w_out[:, c * DIM:(c + 1) * DIM], c == 0, c == chunks - 1),
                                     [rows_done, tile.free, weights["w_out"]], "proj")
                dst = resid[:, b].rearrange("p t f -> p (t f)")
                added = dve.do(lambda e: e.tensor_tensor(dst, tile.buf[:, :], dst, ALU.add), [last, resid_done[b]], "resid")
                wide.give(tile, added)
                finish("w_out", s, last)
                return last, added

            def in_turns(steps, softmax, normalise, turn, mix, prepare=None, start=None):
                steps = list(steps)
                begun = weighed = turned = None
                for k in range(len(steps) + (2 if start is None else 3)):
                    if k < len(steps) and prepare is not None and prepare(steps[k]) is not None:
                        yield []
                    if start is None:
                        scored = softmax(steps[k]) if k < len(steps) else None
                    else:
                        before, begun = begun, start(steps[k]) if k < len(steps) else None
                    yield [turned[-1] if turned is not None else [], weighed[-1] if weighed is not None else []]
                    if turned is not None:
                        mix(*turned)
                    turned = turn(*weighed) if weighed is not None else None
                    yield before[-1] if start is not None and before is not None else []
                    if start is not None:
                        scored = softmax(*before) if before is not None else None
                    yield scored[-1] if scored is not None else []
                    weighed = normalise(*scored) if scored is not None else None
                    yield wide.when()

            def local_layer(s, b, stage, is_first, is_last):
                q_t = work[s][:, 0].rearrange("p (c n) -> p c n", c=PAIRS)
                v = work[s][:, 1].rearrange("p (t n) -> p t n", t=TILES)
                o_t = work[s][:, 2].rearrange("p (c n) -> p c n", c=PAIRS)
                k_p = kpad[s][:, :].rearrange("p (c j n) -> p c j n", c=PAIRS, j=2)
                flat_resid = resid[:, b].rearrange("p t f -> p (t f)")
                zero_pads(s, "pairs")
                if is_first:
                    saved = sp.do(lambda e: e.dma_start(d["saved"][b], flat_resid), resid_done[b], f"saved{b}", 16)
                    stats = yield from norm_stats(s, lambda t: [resid[:, b, t, :]], [[resid_done[b], stream_free[s]]])
                    yield [stats, saved]
                    for t in range(TILES):
                        done = normalised(s, t, resid[:, b, t, :], resid[:, b, t, :], [stats, saved])
                    resid_done[b] = [done]
                    saves[b] = saved
                yield resid_done[b]
                ready = to_features(s, lambda t: resid[:, b, t, :], [resid_done[b]], True)
                yield ready
                yield from claim("w_in", stage)
                yield from claim("small", stage)
                heads = lambda a: a.rearrange("p (h e) -> p h e", e=HD)
                halves = lambda a: a.rearrange("p (h u e) -> p h u e", u=2, e=HD // 2)
                final = Ring([x_n[s][:, :, :].rearrange("p t f -> p (t f)"), prob_own[s][:, :]])
                final.slots[0].free, final.slots[1].free = xn_free[s], prob_free[s]

                raw, sines = work[s][:, 2, 0:2 * INNER], work[s][:, 2, 2 * INNER:4 * INNER]
                raw_free, sines_free = [stream_free[s]], [stream_free[s]]

                def rotated(t):
                    out, tile, vtile = final.take(), wide.take(), narrow[s].take()
                    for third, dst in ((0, tile.buf[:, 0:512]), (1, tile.buf[:, 512:1024]), (2, vtile.buf[:, 0:512])):
                        for c in range(FC):
                            last = pe.do(mm(dst, x_t[s][:, c, 1 - c + t * P:1 - c + (t + 1) * P],
                                            w_in[:, c * 3 * INNER + third * INNER:c * 3 * INNER + (third + 1) * INNER],
                                            c == 0, c == FC - 1),
                                         [ready, weights["w_in"], tile.free, vtile.free], "qkv")
                    copied = act.do(lambda e: e.activation(raw, tile.buf[:, :], ACT.Copy),
                                    [last, *raw_free], "raw")
                    squared = act.do(lambda e: e.activation(scratch_buf[:, :], tile.buf[:, :], ACT.Square),
                                     [last, scratch[0].free, scratch[1].free], "square")
                    got_v = act.do(lambda e: e.activation(v[:, t, :], vtile.buf[:, 0:512], ACT.Copy),
                                   [last, stream_free[s]], "v")
                    wide.give(tile, squared)
                    narrow[s].give(vtile, got_v)
                    for z in range(2):
                        part = slice(z * INNER, (z + 1) * INNER)
                        sind = pool.do(lambda e: e.tensor_tensor(
                            halves(sines[:, part]), halves(raw[:, part])[:, :, ::-1, :],
                            rot[:, 2 * z + 1, t, :].rearrange("p (u e) -> p u e", u=2).unsqueeze(1)
                            .to_broadcast([P, HEADS, 2, HD // 2]), ALU.mult),
                            [copied, *sines_free, weights["small"]], "sin")
                        cosd = dve.do(lambda e: e.tensor_tensor(
                            heads(out.buf[:, part]), heads(raw[:, part]),
                            rot[:, 2 * z, t, :].unsqueeze(1).to_broadcast([P, HEADS, HD]), ALU.mult),
                            [copied, out.free, weights["small"]], "cos")
                    raw_free[:] = [sind, cosd]
                    ss, rn = small.take(), small.take()
                    summed = dve.do(lambda e: e.tensor_reduce(ss.buf[:, 0:16], heads(scratch_buf[:, :]), AX, ALU.add),
                                    [squared, ss.free], "ss")
                    scratch[0].free = scratch[1].free = [summed]
                    clipped = dve.do(lambda e: e.tensor_scalar(ss.buf[:, 0:16], ss.buf[:, 0:16], 1e-24, None, ALU.max),
                                     summed, "ss")
                    power = pool.do(lambda e: e.tensor_tensor(rn.buf[:, 0:16], ss.buf[:, 0:16], minus_half[:, 0:16],
                                                              ALU.pow), [clipped, rn.free, consts], "rn")
                    small.give(ss, power)
                    return t, out, rn, sind, cosd, power, got_v, last

                def joined(t, out, rn, sind, cosd, power, got_v, last):
                    total = dve.do(lambda e: e.tensor_tensor(out.buf[:, :], out.buf[:, :], sines, ALU.add),
                                   [cosd, sind], "turned")
                    sines_free[:] = [total]
                    scaled = dve.do(lambda e: e.tensor_tensor(
                        heads(out.buf[:, :]), heads(out.buf[:, :]), rn.buf[:, 0:16].unsqueeze(2)
                        .to_broadcast([P, 16, HD]), ALU.mult), [total, power], "scaled")
                    small.give(rn, scaled)
                    return t, out, scaled, got_v

                def spread_out(t, out, scaled, got_v):
                    tile = wide.take()
                    for z in range(8):
                        last = pe.do(tr(tile.buf[:, z * P:(z + 1) * P], out.buf[:, z * P:(z + 1) * P]),
                                     [scaled, tile.free], "turn")
                    final.give(out, last)
                    packed = tile.buf[:, :].rearrange("p (z c n) -> p z c n", z=2, c=PAIRS)
                    got_q = act.do(lambda e: e.activation(q_t[:, :, t * P:(t + 1) * P], packed[:, 0], ACT.Copy),
                                   [last, stream_free[s]], "q_t")
                    for j in range(2):
                        r = slice(64 * j, 64 * j + 64)
                        got_k = dve.do(lambda e: e.tensor_copy(k_p[r, :, j, t * P:(t + 1) * P], packed[r, 1]),
                                       [last, stream_free[s], kpad_zero[s]], "k_t")
                    wide.give(tile, got_q, got_k)
                    return [got_q, got_k, got_v]

                ready_out, before = [], None
                for t in range(TILES + 1):
                    now = rotated(t) if t < TILES else None
                    if before is not None:
                        yield before[-2]
                        ready_out = spread_out(*before)
                    if now is not None:
                        yield now[3:6]
                        last_in = now[-1]
                        now = joined(*now)
                    yield wide.when()
                    before = now
                finish("w_in", s, last_in)
                prob_free[s], xn_free[s] = final.slots[1].free, final.slots[0].free
                ready = ready_out
                yield ready
                out_marks = []
                held = Ring([prob_own[s], x_n[s][:, :, :].rearrange("p t f -> p (t f)")])
                held.slots[0].free, held.slots[1].free = prob_free[s], xn_free[s]
                span = lambda t: slice(256 * t + (P if t == 0 else 0), 256 * (t + 1))

                def softmax(h):
                    c, j = h // 2, h % 2
                    tile, st, pr = wide.take(), small.take(), held.take()
                    for t in range(TILES):
                        last = pe.do(mm(tile.buf[:, span(t)], q_t[:, c, t * P:(t + 1) * P],
                                        k_p[:, c, j, P * max(t - 1, 0):(t + 1) * P], True, True),
                                     [ready, tile.free], "score")
                    tables(EXP_TABLES)
                    for t in range(TILES):
                        low = dve.do(lambda e: e.tensor_tensor_reduce(
                            pr.buf[:, span(t)], tile.buf[:, span(t)], local_mask[:, P if t == 0 else 0:256],
                            -1.0, LOW, ALU.add, ALU.min, st.buf[:, t:t + 1]),
                            [last, pr.free, st.free, consts], "max")
                        done = act.do(lambda e: e.activation(
                            pr.buf[:, span(t)], pr.buf[:, span(t)], ACT.Exp, bias=st.buf[:, t:t + 1], scale=-1.0,
                            accum_out=st.buf[:, 4 + t:5 + t]), low, "exp")
                    wide.give(tile, low)
                    return h, pr, st, done

                def normalise(h, pr, st, done):
                    inv = dve.do(lambda e: e.reciprocal(st.buf[:, 8:12], st.buf[:, 4:8]), done, "inv")
                    for t in range(TILES):
                        scaled = pool.do(lambda e: e.tensor_scalar(
                            pr.buf[:, span(t)], pr.buf[:, span(t)], st.buf[:, 8 + t:9 + t], 1.0,
                            ALU.mult, ALU.mult), [inv, done], "weight")
                    small.give(st, scaled)
                    return h, pr, scaled

                def turn(h, pr, scaled):
                    tile, pt = wide.take(), prob_t[s].take()
                    for kb in range(TILES):
                        for t in range(kb, min(kb + 2, TILES)):
                            col = 256 * t + (P if t == kb else 0)
                            last = pe.do(tr(tile.buf[:, 256 * kb + P * (t - kb):256 * kb + P * (t - kb + 1)],
                                            pr.buf[:, col:col + P]), [scaled, tile.free], "turn")
                    held.give(pr, last)
                    got1 = act.do(lambda e: e.activation(pt.buf[:, 0:512], tile.buf[:, 0:512], ACT.Copy),
                                  [last, pt.free], "prob_t")
                    got2 = dve.do(lambda e: e.tensor_copy(pt.buf[:, 512:896], tile.buf[:, 512:896]),
                                  [last, pt.free], "prob_t")
                    wide.give(tile, got1, got2)
                    return h, pt, [got1, got2]

                def mix(h, pt, turned):
                    c, j = h // 2, h % 2
                    if j == 0:
                        o_tiles.append(narrow[s].take())
                    o_tile = o_tiles[-1]
                    for kb in range(TILES):
                        n = P * min(2, TILES - kb)
                        last = pe.do(mm(o_tile.buf[64 * j:64 * j + 64, P * kb:P * kb + n],
                                        v[:, kb, h * HD:(h + 1) * HD], pt.buf[:, 256 * kb:256 * kb + n],
                                        kb == 0, kb == TILES - 1), [turned, o_tile.free], "mix")
                    prob_t[s].give(pt, last)
                    if j == 1:
                        done = act.do(lambda e: e.activation(o_t[:, c, :], o_tile.buf[:, :], ACT.Copy),
                                      [last, stream_free[s]], "o_t")
                        narrow[s].give(o_tile, done)
                        out_marks.append(done)

                o_tiles = []
                yield from in_turns(range(HEADS), softmax, normalise, turn, mix)
                prob_free[s], xn_free[s] = held.slots[0].free, held.slots[1].free
                yield from claim("w_out", stage)
                yield out_marks
                o_read, added = project_out(s, b, lambda c: o_t[:, c, :], PAIRS, out_marks)
                resid_done[b] = [added]
                yield added
                moved = [
                    sp.do(lambda e: e.dma_start(shifted[s][1:P, :, :], resid[0:P - 1, b, :, P:DIM]),
                          [added, shift_free[s]], f"shift{s}", 16),
                    sp.do(lambda e: e.dma_start(shifted[s][0:1, 1:TILES, :], resid[P - 1:P, b, 0:TILES - 1, P:DIM]),
                          [added, shift_free[s]], f"shift{s}", 16)]
                stats = yield from norm_stats(s, lambda t: [resid[:, b, t, 0:P], shifted[s][:, t, :]],
                                   [added, [added, moved[-1], consts]])
                yield stats
                for t in range(TILES):
                    normalised(s, t, x_n[s][:, t, 0:P], resid[:, b, t, 0:P], [stats, xn_free[s]])
                    done = normalised(s, t, x_n[s][:, t, P:DIM], shifted[s][:, t, :], [stats, xn_free[s]])
                shift_free[s] = [done]
                biased = pool.do(lambda e: e.tensor_tensor(
                    resid[:, b], resid[:, b], bias_row[:, :].unsqueeze(1).to_broadcast([P, TILES, DIM]), ALU.add),
                    [done, added, weights["small"]], "bias")
                resid_done[b] = [biased]
                yield done
                ready = to_features(s, lambda t: x_n[s][:, t, :], [done], False, weights["small"])
                xn_free[s] = ready
                act_in = work[s][:, :, :].rearrange("p a n -> p (a n)")
                gate = act_in[:, 0:HC * TOKENS].rearrange("p (m n) -> p m n", m=HC)
                hidden = act_in[:, HC * TOKENS:2 * HC * TOKENS].rearrange("p (m n) -> p m n", m=HC)
                blank = pool.do(lambda e: e.memset(hidden[:, HC - 1, :], 0.0), [o_read], "blank")
                yield from claim("w_up", stage)
                yield ready

                def up(part, m):
                    n = P if m < HC - 1 else HLAST
                    return [(lambda dst, c=c: mm(dst, w_up[:, c, part * HID + m * P:part * HID + m * P + n],
                                                 x_t[s][:, c, 1:1 + TOKENS], c == 0, c == FC - 1)) for c in range(FC)], n

                for m0 in range(0, HC, 2):
                    tile = wide.take()
                    for m in (m0, m0 + 1):
                        steps, n = up(1, m)
                        dst = tile.buf[0:n, (m - m0) * 512:(m - m0) * 512 + 512]
                        for one in steps:
                            last = pe.do(one(dst), [ready, weights["w_up"], tile.free], "up")
                        got = dve.do(lambda e, m=m, n=n, dst=dst: e.tensor_scalar(
                            gate[0:n, m, :], dst, bias_up[0:n, HC + m:HC + m + 1], None, ALU.add),
                            [last, o_read, weights["small"]], "gate")
                    wide.give(tile, got)
                    yield wide.when()
                tables(GELU_TABLES)
                act.do(lambda e: e.activation(gate[:, 0:HC - 1, :], gate[:, 0:HC - 1, :], ACT.Gelu), got, "gelu")
                gated = act.do(lambda e: e.activation(gate[0:HLAST, HC - 1, :], gate[0:HLAST, HC - 1, :], ACT.Gelu),
                               got, "gelu")
                for m0 in range(0, HC, 2):
                    tile = wide.take()
                    for m in (m0, m0 + 1):
                        steps, n = up(0, m)
                        dst = tile.buf[0:n, (m - m0) * 512:(m - m0) * 512 + 512]
                        for one in steps:
                            last = pe.do(one(dst), [ready, tile.free], "up")
                        got = dve.do(lambda e, m=m, n=n, dst=dst: e.scalar_tensor_tensor(
                            out=hidden[0:n, m, :], in0=dst, scalar=bias_up[0:n, m:m + 1], in1=gate[0:n, m, :],
                            op0=ALU.add, op1=ALU.mult), [last, gated, blank], "hidden")
                    wide.give(tile, got)
                    yield wide.when()
                finish("w_up", s, last)
                yield from claim("w_down", stage)
                yield got
                tile = wide.take()
                for t in range(TILES):
                    for m in range(HC):
                        last = pe.do(mm(tile.buf[:, t * DIM:(t + 1) * DIM], hidden[:, m, t * P:(t + 1) * P],
                                        w_down[:, m, :], m == 0, m == HC - 1),
                                     [got, tile.free, weights["w_down"]], "down")
                finish("w_down", s, last)
                added = dve.do(lambda e: e.tensor_tensor(flat_resid, tile.buf[:, :], flat_resid, ALU.add),
                               [last, biased], "resid")
                wide.give(tile, added)
                finish("small", s, [added, ready])
                resid_done[b] = [added]
                stream_free[s] = [last, got]
                if is_last:
                    back = x_n[s][:, :, :].rearrange("p t f -> p (t f)")
                    loaded = load(back, d["saved"][b], [xn_free[s], saves[b]], f"back{s}")
                    yield []
                    added = pool.do(lambda e: e.tensor_tensor(flat_resid, flat_resid, back, ALU.add),
                                    [loaded, added], "resid")
                    xn_free[s] = [added]
                    resid_done[b] = [added]
                yield []

            def attention_a(s, b, stage):
                q_t = work[s][:, 0].rearrange("p (c n) -> p c n", c=PAIRS)
                v = work[s][:, 1].rearrange("p (t n) -> p t n", t=TILES)
                o_t = work[s][:, 2].rearrange("p (c n) -> p c n", c=PAIRS)
                k_p = kpad[s][:, :].rearrange("p (c j n) -> p c j n", c=PAIRS, j=2)
                wq = w_in[:, 0:2 * INNER].rearrange("p (c n) -> p c n", c=FC)
                wd = w_in[:, 1024:1024 + FC * RANK].rearrange("p (c n) -> p c n", c=FC)
                wk, wv = w_in[:, 1152:1664], w_in[:, 1664:2176]
                zero_pads(s, "pairs")
                yield from claim("w_in", stage)
                stats = yield from norm_stats(s, lambda t: [resid[:, b, t, :]], [[resid_done[b], stream_free[s]]])
                yield stats
                for t in range(TILES):
                    done = normalised(s, t, x_n[s][:, t, :], resid[:, b, t, :], [stats, xn_free[s]])
                yield done
                ready = to_features(s, lambda t: x_n[s][:, t, :], [done], False)
                xn_free[s] = ready
                yield ready
                for c0 in range(0, PAIRS, 2):
                    tile = wide.take()
                    for c in (c0, c0 + 1):
                        for k in range(FC):
                            last = pe.do(mm(tile.buf[:, (c - c0) * 512:(c - c0) * 512 + 512], wq[:, k, c * P:(c + 1) * P],
                                            x_t[s][:, k, 1:1 + TOKENS], k == 0, k == FC - 1),
                                         [ready, weights["w_in"], tile.free], "qkv")
                    got_q = act.do(lambda e, c0=c0, tile=tile: e.activation(
                        q_t[:, c0:c0 + 2, :].rearrange("p c n -> p (c n)"), tile.buf[:, :], ACT.Copy, scale=HD ** -0.5),
                        [last, stream_free[s]], "q_t")
                    wide.give(tile, got_q)
                latent = x_n[s][:, 0:2, :].rearrange("p a n -> p (a n)")
                tile = wide.take()
                for k in range(FC):
                    last = pe.do(mm(tile.buf[0:RANK, 0:512], wd[:, k, :], x_t[s][:, k, 1:1 + TOKENS], k == 0, k == FC - 1),
                                 [tile.free], "qkv")
                blank = dve.do(lambda e: e.memset(latent[RANK:P, :], 0.0), ready, "blank")
                got = act.do(lambda e: e.activation(latent[0:RANK, :], tile.buf[0:RANK, 0:512], ACT.Copy),
                             [last, ready], "latent")
                wide.give(tile, got)
                yield []
                for c0 in range(0, PAIRS, 2):
                    tile = wide.take()
                    for c in (c0, c0 + 1):
                        last = pe.do(mm(tile.buf[:, (c - c0) * 512:(c - c0) * 512 + 512], wk[:, c * P:(c + 1) * P],
                                        latent, True, True), [got, blank, tile.free], "qkv")
                    for j in range(2):
                        r = slice(64 * j, 64 * j + 64)
                        got_k = dve.do(lambda e, c0=c0, j=j, r=r, tile=tile: e.tensor_copy(
                            k_p[r, c0:c0 + 2, j, :], tile.buf[r, :].rearrange("p (c n) -> p c n", c=2)),
                            [last, stream_free[s], kpad_zero[s]], "k_t")
                    wide.give(tile, got_k)
                    tile = wide.take()
                    for t in (c0, c0 + 1):
                        last = pe.do(mm(tile.buf[:, (t - c0) * 512:(t - c0) * 512 + 512], latent[:, t * P:(t + 1) * P],
                                        wv, True, True), [got, blank, tile.free], "qkv")
                    got_v = act.do(lambda e, c0=c0, tile=tile: e.activation(
                        v[:, c0:c0 + 2, :].rearrange("p c n -> p (c n)"), tile.buf[:, :], ACT.Copy),
                        [last, stream_free[s]], "v")
                    wide.give(tile, got_v)
                    yield []
                xn_free[s] = [last]
                finish("w_in", s, last)
                ready = [got_q, got_k, got_v]
                yield from claim("w_up", stage)
                out_marks = []
                held = Ring([prob_own[s], spare(s)])
                held.slots[0].free, held.slots[1].free = prob_free[s], spare_free[s]

                def softmax(step):
                    h, half = step
                    c, j = h // 2, h % 2
                    tile, st, pr = wide.take(), small.take(), held.take()
                    for i in range(2):
                        t = 2 * half + i
                        last = pe.do(mm(tile.buf[:, i * 512:i * 512 + 512], q_t[:, c, t * P:(t + 1) * P],
                                        k_p[:, c, j, :], True, True), [ready, tile.free], "score")
                    low = dve.do(lambda e: e.tensor_reduce(
                        st.buf[:, 0:2], tile.buf[:, :].rearrange("p (t n) -> p t n", t=2), AX, ALU.max,
                        negate=True), [last, st.free], "max")
                    tables(EXP_TABLES)
                    for i in range(2):
                        cut = slice(i * 512, i * 512 + 512)
                        done = act.do(lambda e: e.activation(
                            pr.buf[:, cut], tile.buf[:, cut], ACT.Exp, bias=st.buf[:, i:i + 1],
                            accum_out=st.buf[:, 2 + i:3 + i]), [low, pr.free], "exp")
                    wide.give(tile, done)
                    return step, pr, st, done

                def normalise(step, pr, st, done):
                    inv = dve.do(lambda e: e.reciprocal(st.buf[:, 4:6], st.buf[:, 2:4]), done, "inv")
                    marks = []
                    for i, queue in ((0, pool), (1, dve)):
                        cut = slice(i * 512, i * 512 + 512)
                        marks.append(queue.do(lambda e: e.tensor_scalar(
                            pr.buf[:, cut], pr.buf[:, cut], st.buf[:, 4 + i:5 + i], 1.0,
                            ALU.mult, ALU.mult), [inv, done], "weight"))
                    small.give(st, marks)
                    return step, pr, marks

                def turn(step, pr, scaled):
                    tile, pt = wide.take(), prob_t[s].take()
                    for kb in range(TILES):
                        for i in range(2):
                            last = pe.do(tr(tile.buf[:, kb * 256 + i * P:kb * 256 + (i + 1) * P],
                                            pr.buf[:, i * 512 + kb * P:i * 512 + (kb + 1) * P]),
                                         [scaled, tile.free], "turn")
                    held.give(pr, last)
                    got1 = act.do(lambda e: e.activation(pt.buf[:, 0:512], tile.buf[:, 0:512], ACT.Copy),
                                  [last, pt.free], "prob_t")
                    got2 = dve.do(lambda e: e.tensor_copy(pt.buf[:, 512:1024], tile.buf[:, 512:1024]),
                                  [last, pt.free], "prob_t")
                    wide.give(tile, got1, got2)
                    return step, pt, [got1, got2]

                def mix(step, pt, turned):
                    h, half = step
                    c, j = h // 2, h % 2
                    if j == half == 0:
                        o_tiles.append(narrow[s].take())
                    o_tile = o_tiles[-1]
                    for kb in range(TILES):
                        last = pe.do(mm(o_tile.buf[64 * j:64 * j + 64, 256 * half:256 * half + 256],
                                        v[:, kb, h * HD:(h + 1) * HD], pt.buf[:, kb * 256:kb * 256 + 256],
                                        kb == 0 and half == 0, kb == TILES - 1),
                                     [turned, o_tile.free], "mix")
                    prob_t[s].give(pt, last)
                    if j == 1 and half == 1:
                        done = act.do(lambda e: e.activation(o_t[:, c, :], o_tile.buf[:, :], ACT.Copy),
                                      [last, stream_free[s]], "o_t")
                        narrow[s].give(o_tile, done)
                        out_marks.append(done)

                o_tiles = []
                yield from in_turns([(h, half) for h in range(HEADS) for half in range(2)],
                                    softmax, normalise, turn, mix)
                prob_free[s], spare_free[s] = held.slots[0].free, held.slots[1].free
                finish("w_up", s, spare_free[s])
                yield from claim("w_out", stage)
                o_read, added = project_out(s, b, lambda c: o_t[:, c, :], PAIRS, out_marks)
                resid_done[b] = [added]
                stream_free[s] = [o_read]
                yield []

            def attention_causal(s, b, stage):
                q_a = work[s][:, 0].rearrange("p (g t n) -> p g t n", g=GROUPS, t=TILES)
                k_a = work[s][:, 1].rearrange("p (g t n) -> p g t n", g=GROUPS, t=TILES)
                v = work[s][:, 2].rearrange("p (t n) -> p t n", t=TILES)
                q_rows, qd_rows = (x_t[s][:, i, 1:1 + TOKENS] for i in range(2))
                k_rows = scratch[s].buf
                k_p = kpad[s][:, :].rearrange("p (o h n) -> p o h n", o=2, h=4)
                w = w_in[:, 0:FC * 3 * DIM].rearrange("p (c n) -> p c n", c=FC)
                zero_pads(s, "fours")
                yield from claim("w_in", stage)
                yield from claim("small", stage)
                yield from claim("w_up", stage)
                yield from claim("w_down", stage)
                stats = yield from norm_stats(s, lambda t: [resid[:, b, t, :]], [[resid_done[b], stream_free[s]]])
                yield stats
                for t in range(TILES):
                    done = normalised(s, t, x_n[s][:, t, :], resid[:, b, t, :], [stats, xn_free[s]])
                biased = pool.do(lambda e: e.tensor_tensor(
                    resid[:, b], resid[:, b], bias_row[:, :].unsqueeze(1).to_broadcast([P, TILES, DIM]), ALU.add),
                    [done, resid_done[b], weights["small"]], "bias")
                resid_done[b] = [biased]
                blank = [pool.do(lambda e, i=i: e.memset(work[s][:, i, :], 0.0), stream_free[s], "blank") for i in range(3)]
                rows4 = lambda a: a.rearrange("p g t (h e) -> p (g t) h e", e=BROW)
                pool.do(lambda e: e.memset(rows4(q_a)[:, :, :, BHD + 1:BHD + 2], 1.0), blank, "blank")
                blank = pool.do(lambda e: e.memset(rows4(k_a)[:, :, :, BHD:BHD + 1], 1.0), blank, "blank")
                yield done
                ready = to_features(s, lambda t: x_n[s][:, t, :], [done], False)
                xn_free[s] = ready
                yield ready
                ends = []
                for t in range(TILES):
                    tile = wide.take()
                    for c in range(FC):
                        for lo, n in ((0, 512), (512, 256)):
                            last = pe.do(mm(tile.buf[:, lo:lo + n], x_t[s][:, c, 1 + t * P:1 + (t + 1) * P],
                                            w[:, c, lo:lo + n], c == 0, c == FC - 1),
                                         [ready, weights["w_in"], tile.free], "qkv")
                    row = Slot(spare(s))
                    got = dve.do(lambda e, tile=tile, row=row: e.tensor_tensor(
                        row.buf[:, 0:3 * DIM], tile.buf[:, 0:3 * DIM], qkv_bias, ALU.add),
                        [last, spare_free[s], weights["small"]], "raw")
                    wide.give(tile, got)
                    sq, ss, sk = prob_own[s], small.take(), small.take()
                    squared = act.do(lambda e, row=row, sq=sq: e.activation(
                        sq[:, 0:2 * DIM], row.buf[:, 0:2 * DIM], ACT.Square), [got, prob_free[s]], "square")
                    for z, one in ((0, ss), (1, sk)):
                        summed = dve.do(lambda e, z=z, one=one, sq=sq: e.tensor_reduce(
                            one.buf[:, 0:16], sq[:, z * DIM:(z + 1) * DIM].rearrange("p (h e) -> p h e", e=BHD),
                            AX, ALU.add), [squared, one.free], "ss")
                    prob_free[s] = [summed]
                    head = lambda a: a.rearrange("p (g h e) -> p g h e", g=GROUPS, e=BHD)
                    slot = lambda a, t, lo, n: a[:, :, t, :].rearrange("p g (h e) -> p g h e", e=BROW)[:, :, :, lo:lo + n]
                    one4 = lambda a: a[:, 0:16].rearrange("p (g h e) -> p g h e", g=GROUPS, e=1)
                    w1 = pool.do(lambda e, t=t, row=row: e.tensor_scalar(slot(q_a, t, 0, BHD), head(row.buf[:, 0:DIM]),
                                                                         -2.0, 1.0, ALU.mult, ALU.mult), [got, blank], "rows")
                    w2 = pool.do(lambda e, t=t, row=row: e.tensor_scalar(slot(k_a, t, 0, BHD), head(row.buf[:, DIM:2 * DIM]),
                                                                         1.0, 1.0, ALU.mult, ALU.mult), [got, blank], "rows")
                    w3 = pool.do(lambda e, t=t, ss=ss: e.tensor_scalar(slot(q_a, t, BHD, 1), one4(ss.buf), EPS_B, 1.0,
                                                                       ALU.add, ALU.mult), [summed, blank], "rows")
                    w4 = pool.do(lambda e, t=t, sk=sk: e.tensor_scalar(slot(k_a, t, BHD + 1, 1), one4(sk.buf), 1.0, 1.0,
                                                                       ALU.mult, ALU.mult), [summed, blank], "rows")
                    w5 = act.do(lambda e, t=t, row=row: e.activation(
                        v[:, t, :].rearrange("p (h e) -> p h e", e=BROW)[:, :, 0:BHD],
                        row.buf[:, 2 * DIM:3 * DIM].rearrange("p (h e) -> p h e", e=BHD), ACT.Copy), [got, blank], "v")
                    spare_free[s] = [squared, w4, w5]
                    small.give(ss, w4)
                    small.give(sk, w4)
                    ends = [w4, w5]
                    yield []
                qkv_read = last
                finish("w_in", s, [last, got])
                out_marks = []
                few = lambda a, i: a[:, i * FEW:(i + 1) * FEW]
                held = [Ring([few(w_down_flat, 2 * s), few(w_down_flat, 2 * s + 1)]), Ring([prob_own[s], spare(s)])]
                held[1].slots[0].free, held[1].slots[1].free = prob_free[s], spare_free[s]
                inverse = [Ring([few(rot_flat, s)]), Ring([x_n[s][:, :, :].rearrange("p t f -> p (t f)")])]
                denominator = [Ring([shifted[s][:, 1:TILES, :].rearrange("p t f -> p (t f)")]), Ring([rows[:, s, :]])]
                inverse[1].slots[0].free = xn_free[s]
                inverse[0].slots[0].free = few_free[s]
                for one in held[0].slots:
                    one.free = few_free[s]
                denominator[0].slots[0].free = shift_free[s]
                denominator[1].slots[0].free = rows_free[s]
                o_tiles, rows_done, keys_done = [], [], []
                def group_keys(g):
                    tile, o = wide.take(), g % 2
                    for t in range(TILES):
                        last = pe.do(tr(tile.buf[:, t * P:(t + 1) * P], k_a[:, g, t, :]), [ends, tile.free], "turn")
                    got = act.do(lambda e: e.activation(k_rows, tile.buf[:, 0:512], ACT.Copy),
                                 [last, spread_last[s], scratch[s].free], "k_t")
                    wide.give(tile, got)
                    for j in range(4):
                        spread = load(k_p[32 * j:32 * j + 32, o, j, :], k_rows[32 * j:32 * j + 32, :],
                                      [got, kpad_zero[s], pad_free[s][o]], f"spread{s}")
                    spread_last[s] = keys_done[:] = [spread]

                def group_queries(g):
                    tile = wide.take()
                    for t in range(TILES):
                        last = pe.do(tr(tile.buf[:, t * P:(t + 1) * P], q_a[:, g, t, :]), [ends, tile.free], "turn")
                    a1 = act.do(lambda e: e.activation(q_rows, tile.buf[:, 0:512], ACT.Copy),
                                [last, group_free[s], qkv_read], "q_t")
                    a2 = dve.do(lambda e: e.tensor_scalar(qd_rows, tile.buf[:, 0:512], dot_rows[:, 0:1], None,
                                                          ALU.mult), [a1, group_free[s], qkv_read, consts], "q_t")
                    wide.give(tile, a1, a2)
                    rows_done[:] = [a1, a2, *keys_done]

                def prepare(step):
                    g, j, half = step
                    if step == (0, 0, 0):
                        group_keys(0)
                    if j == half == 0:
                        group_queries(g)
                        return True
                    if (j, half) == (2, 0) and g + 1 < GROUPS:
                        group_keys(g + 1)
                        return True
                    return None

                def spans(half):
                    n = [P * (2 * half + i + 1) for i in range(2)]
                    return n, [slice(0, n[0]), slice(n[0], n[0] + n[1])], slice(0, n[0] + n[1])

                def start(step):
                    g, j, half = step
                    o = g % 2
                    st, pr, dn, inv_t = small.take(), held[half].take(), denominator[half].take(), inverse[half].take()
                    tables(EXP_TABLES)
                    n, cuts, both = spans(half)
                    dens = wide.take()
                    if half == 0:
                        dots, den_at, dot_at = dens, [512, 512 + n[0]], [0, n[0]]
                    else:
                        dots, den_at, dot_at = wide.take(), [512 - n[0], 512], [512 - n[0], 512]
                    for i in range(2):
                        t = 2 * half + i
                        last = pe.do(mm(dens.buf[:, den_at[i]:den_at[i] + n[i]], q_rows[:, t * P:(t + 1) * P],
                                        k_p[:, o, j, 0:n[i]], True, True), [rows_done, dens.free], "score")
                    for i in range(2):
                        t = 2 * half + i
                        dot = pe.do(mm(dots.buf[:, dot_at[i]:dot_at[i] + n[i]], qd_rows[:, t * P:(t + 1) * P],
                                       k_p[:, o, j, 0:n[i]], True, True), [rows_done, dots.free], "score")
                    group_free[s] = pad_free[s][o] = [dot]
                    den = dve.do(lambda e: e.tensor_scalar(dn.buf[:, both], dens.buf[:, den_at[0]:den_at[1] + n[1]],
                                                           DEN_MIN, DEN_MAX, ALU.max, ALU.min), [last, dn.free], "den")
                    num = act.do(lambda e: e.activation(pr.buf[:, both], dots.buf[:, dot_at[0]:dot_at[1] + n[1]],
                                                        ACT.Square, scale=0.5), [dot, pr.free], "square")
                    logs = act.do(lambda e: e.activation(inv_t.buf[:, both], dn.buf[:, both], ACT.Ln),
                                  [den, inv_t.free], "ln")
                    guess = act.do(lambda e: e.activation(inv_t.buf[:, both], inv_t.buf[:, both], ACT.Exp, scale=-1.0),
                                   logs, "guess")
                    wide.give(dens, den, num)
                    if dots is not dens:
                        wide.give(dots, num)
                    close = pool.do(lambda e: e.tensor_tensor(dn.buf[:, both], dn.buf[:, both], inv_t.buf[:, both],
                                                              ALU.mult), guess, "close")
                    return step, st, pr, dn, inv_t, num, close

                def softmax(step, st, pr, dn, inv_t, num, close):
                    g, j, half = step
                    n, cuts, both = spans(half)
                    inv = dve.do(lambda e: e.scalar_tensor_tensor(
                        out=inv_t.buf[:, both], in0=dn.buf[:, both], scalar=2.0, in1=inv_t.buf[:, both],
                        op0=ALU.subtract, op1=ALU.mult), close, "inv")
                    denominator[half].give(dn, inv)
                    for i in range(2):
                        own = slice(cuts[i].stop - P, cuts[i].stop)
                        early = slice(cuts[i].start, cuts[i].stop - P)
                        high = st.free
                        if n[i] > P:
                            high = dve.do(lambda e: e.tensor_tensor_reduce(
                                pr.buf[:, early], pr.buf[:, early], inv_t.buf[:, early], -1.0, -LOW,
                                ALU.mult, ALU.max, st.buf[:, 8 + i:9 + i]), [num, inv, st.free], "max")
                        ratio = dve.do(lambda e: e.scalar_tensor_tensor(
                            out=pr.buf[:, own], in0=pr.buf[:, own], scalar=-1.0, in1=inv_t.buf[:, own],
                            op0=ALU.mult, op1=ALU.mult), [num, inv], "ratio")
                        low = dve.do(lambda e: e.tensor_tensor_reduce(
                            pr.buf[:, own], pr.buf[:, own], causal_mask[:, 0:P], 1.0,
                            st.buf[:, 8 + i:9 + i] if n[i] > P else -LOW, ALU.add, ALU.max, st.buf[:, i:i + 1]),
                            [ratio, high, consts], "max")
                    inverse[half].give(inv_t, ratio)
                    low = dve.do(lambda e: e.tensor_scalar(st.buf[:, 2:4], st.buf[:, 0:2], -1.0, None, ALU.mult),
                                 low, "max")
                    for i in range(2):
                        done = act.do(lambda e: e.activation(
                            pr.buf[:, cuts[i]], pr.buf[:, cuts[i]], ACT.Exp,
                            bias=st.buf[:, 2 + i:3 + i], accum_out=st.buf[:, 4 + i:5 + i]), low, "exp")
                    return step, pr, st, done

                def normalise(step, pr, st, done):
                    g, j, half = step
                    n, cuts, both = spans(half)
                    inv = dve.do(lambda e: e.reciprocal(st.buf[:, 6:8], st.buf[:, 4:6]), done, "inv")
                    for i in range(2):
                        scaled = pool.do(lambda e: e.tensor_scalar(
                            pr.buf[:, cuts[i]], pr.buf[:, cuts[i]], st.buf[:, 6 + i:7 + i],
                            1.0, ALU.mult, ALU.mult), [inv, done], "weight")
                    small.give(st, scaled)
                    return step, pr, scaled

                def turn(step, pr, scaled):
                    g, j, half = step
                    tile, pt = wide.take(), prob_t[s].take()
                    n, cuts, both = spans(half)
                    blocks = [(kb, i) for kb in range(2 * half + 2) for i in range(2) if kb <= 2 * half + i]
                    for kb, i in blocks:
                        last = pe.do(tr(tile.buf[:, kb * 256 + i * P:kb * 256 + (i + 1) * P],
                                        pr.buf[:, cuts[i].start + kb * P:cuts[i].start + (kb + 1) * P]),
                                     [scaled, tile.free], "turn")
                    held[half].give(pr, last)
                    got = []
                    for bank in range(half + 1):
                        pieces = [(512 * bank, 512)] if bank < half else [(512 * bank, 256), (512 * bank + 384, P)]
                        for at, w_ in pieces:
                            got = act.do(lambda e: e.activation(pt.buf[:, at:at + w_], tile.buf[:, at:at + w_],
                                                                ACT.Copy), [last, pt.free], "prob_t")
                    wide.give(tile, got)
                    return step, pt, got

                def mix(step, pt, turned):
                    g, j, half = step
                    h = 4 * g + j
                    if j == half == 0:
                        o_tiles.append(narrow[s].take())
                    o_tile = o_tiles[-1]
                    for kb in range(2 * half + 2):
                        i = 1 if kb == 2 * half + 1 else 0
                        last = pe.do(mm(o_tile.buf[32 * j:32 * j + 32, 256 * half + i * P:256 * half + 256],
                                        v[:, kb, h * BROW:(h + 1) * BROW],
                                        pt.buf[:, kb * 256 + i * P:kb * 256 + 256],
                                        kb == 0 and half == 0, kb == 2 * half + 1), [turned, o_tile.free], "mix")
                    prob_t[s].give(pt, last)
                    if j == 3 and half == 1:
                        out = q_a[:, g].rearrange("p t n -> p (t n)")
                        done = act.do(lambda e: e.activation(out, o_tile.buf[:, :], ACT.Copy), last, "o_t")
                        narrow[s].give(o_tile, done)
                        out_marks.append(done)

                yield from in_turns([(g, j, half) for g in range(GROUPS) for j in range(4) for half in range(2)],
                                    softmax, normalise, turn, mix,
                                    prepare, start)
                rows_free[s] = denominator[1].slots[0].free
                shift_free[s] = denominator[0].slots[0].free
                scratch[s].free = spread_last[s]
                prob_free[s], spare_free[s] = held[1].slots[0].free, held[1].slots[1].free
                xn_free[s] = inverse[1].slots[0].free
                few_free[s] = [held[0].slots[0].free, held[0].slots[1].free, inverse[0].slots[0].free]
                finish("w_up", s, spare_free[s])
                finish("w_down", s, few_free[s])
                finish("small", s, [biased, few_free[s]])
                yield from claim("w_out", stage)
                o_read, added = project_out(s, b, lambda c: q_a[:, c].rearrange("p t n -> p (t n)"), GROUPS, out_marks)
                resid_done[b] = [added]
                stream_free[s] = [o_read]
                yield []

            rows_free = [[], []]
            prob_free, spare_free, spread_last = ([[], []] for _ in range(3))
            shift_free, xn_free, group_free, few_free = ([[], []] for _ in range(4))
            pad_free = [[[], []], [[], []]]
            saves = {}
            kpad_zero = [[], []]
            qkv_bias = w_in[:, 2304:2304 + 3 * DIM]

            def load_weights(name, stage, depth):
                free = flat(list(weight_users[name].values()))
                over = lambda a, c: a.rearrange("p (c n) -> p c n", c=c)
                rows_of = lambda a: a.rearrange("(c p) n -> p c n", p=P)
                if name == "w_up" and stage != "f":
                    for s in range(2):
                        spare_free[s] = free
                elif name == "w_down" and stage == "b":
                    for s in range(2):
                        few_free[s] = [free, flat(list(weight_users["small"].values()))]
                elif name == "w_in" and stage == "a":
                    pads = dve.do(lambda e: e.memset(w_in[RANK:P, 1152:2176], 0.0), free, "wpad")
                    load(over(w_in[:, 0:1024], FC), rows_of(d["a_wq_t"]), free, name)
                    load(over(w_in[:, 1024:1152], FC), rows_of(d["a_wd_t"]), free, name)
                    load(w_in[0:RANK, 1152:1664], d["a_wk_t"], free, name)
                    weights[name] = [load(w_in[0:RANK, 1664:2176], d["a_wv_t"], free, name), pads]
                elif name == "w_out" and stage == "a":
                    weights[name] = [load(over(w_out[:, :], PAIRS), rows_of(d["a_wo_t"]), free, name)]
                elif name == "w_in" and stage == "b":
                    load(over(w_in[:, 0:FC * 3 * DIM], FC), rows_of(d["b_wqkv"]), free, name)
                    weights[name] = [load(qkv_bias, d["b_bqkv"].unsqueeze(0).to_broadcast([P, 3 * DIM]), free, name)]
                elif name == "w_out" and stage == "b":
                    zero = pool.do(lambda e: e.memset(w_out[:, :], 0.0), free, "wpad")
                    for j in range(4):
                        last = load(over(w_out[32 * j:32 * j + BHD, :], GROUPS),
                                    d["b_wout"].rearrange("(g j e) n -> j e g n", g=GROUPS, e=BHD)[j], zero, name)
                    weights[name] = [last]
                elif name == "small" and stage == "b":
                    weights[name] = [load(bias_row[:, :], d["b_bout"].unsqueeze(0).to_broadcast([P, DIM]), free, name),
                                     weights["w_in"]]
                elif name == "w_in":
                    weights[name] = [load(over(w_in[:, :], FC), rows_of(d["f_wqkv"][depth]), free, name)]
                elif name == "w_out":
                    weights[name] = [load(over(w_out[:, :], PAIRS), rows_of(d["f_wo"][depth]), free, name)]
                elif name == "w_up":
                    weights[name] = [load(w_up[:, :, :], rows_of(d["f_w1"][depth]), free, name)]
                elif name == "w_down":
                    zero = pool.do(lambda e: e.memset(w_down[:, HC - 1, :], 0.0), free, "wpad")
                    load(w_down[:, 0:HC - 1, :], rows_of(d["f_w2"][depth, 0:(HC - 1) * P]), free, name)
                    weights[name] = [load(w_down[0:HLAST, HC - 1, :], d["f_w2"][depth, (HC - 1) * P:HID], zero, name)]
                else:
                    load(rot[:, :, :, :], d["rotary"], free, name)
                    load(qk_scale[:, 0, :], d["f_qs"][depth].unsqueeze(0).to_broadcast([P, HD]), free, name)
                    load(qk_scale[:, 1, :], d["f_ks"][depth].unsqueeze(0).to_broadcast([P, HD]), free, name)
                    load(ln_gb[:, 0, :], d["f_lg"][depth].rearrange("(c p) -> p c", p=P), free, name)
                    load(ln_gb[:, 1, :], d["f_lb"][depth].rearrange("(c p) -> p c", p=P), free, name)
                    for part in range(2):
                        lo = part * HID
                        load(bias_up[:, part * HC:part * HC + HC - 1],
                             d["f_b1"][depth, lo:lo + (HC - 1) * P].rearrange("(c p) -> p c", p=P), free, name)
                        load(bias_up[0:HLAST, part * HC + HC - 1:part * HC + HC],
                             d["f_b1"][depth, lo + (HC - 1) * P:lo + HID].unsqueeze(1), free, name)
                    last = load(bias_row[:, :], d["f_b2"][depth].unsqueeze(0).to_broadcast([P, DIM]), free, name)
                    for z in range(2):
                        whole = qk_scale[:, z, :].unsqueeze(1).to_broadcast([P, TILES, HD])
                        swap = qk_scale[:, z, :].rearrange("p (u e) -> p u e", u=2)[:, ::-1, :].unsqueeze(1)\
                            .to_broadcast([P, TILES, 2, HD // 2])
                        pool.do(lambda e: e.tensor_tensor(rot[:, 2 * z], rot[:, 2 * z], whole, ALU.mult), last, "tables")
                        table = rot[:, 2 * z + 1].rearrange("p t (u e) -> p t u e", u=2)
                        made = pool.do(lambda e: e.tensor_tensor(table, table, swap, ALU.mult), last, "tables")
                    weights[name] = [made, last]

            holds, pending = {}, {}

            def claim(name, n):
                while holds.get(name) != n:
                    if pending.get(name, 0):
                        yield BLOCKED
                    else:
                        load_weights(name, *PLAN[n])
                        holds[name], pending[name] = n, SEQS

            def finish(name, s, marks):
                weight_users[name][s] = flat(marks)
                pending[name] -= 1

            def spare(s):
                return w_up[:, :, :].rearrange("p c n -> p (c n)")[:, s * 1024:(s + 1) * 1024]

            pad_kind = [None, None]

            def zero_pads(s, kind):
                if pad_kind[s] != kind:
                    pad_kind[s] = kind
                    kpad_zero[s] = [pool.do(lambda e: e.memset(kpad[s][:, :], 0.0),
                                            [stream_free[s], pad_free[s]], "kpad")]

            def unit(n, b):
                stage, depth = PLAN[n]
                if stage == "a":
                    return lambda s: attention_a(s, b, n)
                if stage == "b":
                    return lambda s: attention_causal(s, b, n)
                return lambda s: local_layer(s, b, n, depth == 0, depth == DEPTH - 1)

            waiting = [unit(n, b) for n in range(len(PLAN)) for b in range(SEQS)]
            flying, places = [], [0, 1]
            while waiting or flying:
                while waiting and places:
                    s = places.pop(0)
                    flying.append([s, waiting.pop(0)(s), []])
                item = next((i for i in flying if when(i[2]) <= pe.clock), None) or \
                    min(flying, key=lambda i: when(i[2]))
                flying.remove(item)
                marks = next(item[1], "end")
                if marks == "end":
                    places.append(item[0])
                else:
                    item[2] = marks
                    flying.append(item)
            stored = [sp.do(lambda e, b=b: e.dma_start(d["out"][b].rearrange("(t p) f -> p t f", p=P), resid[:, b]),
                            resid_done[b], "out", 16) for b in range(SEQS)]
            sp.wait(stored[-1])

        block = stack.enter_context(nc.Block())
        for live in ("tensor", "scalar", "vector", "gpsimd", "sync"):
            engine_block = {"tensor": block.tensor, "scalar": block.scalar, "vector": block.vector,
                            "gpsimd": block.gpsimd, "sync": block.sync}[live]
            engine_block(lambda eng, live=live: schedule(live, eng))


COSTS = {
    ("pe", "turn"): 0.11, ("pe", "qkv"): 0.86, ("pe", "score"): 0.43, ("pe", "mix"): 0.16, ("pe", "proj"): 0.43,
    ("pe", "up"): 0.86, ("pe", "down"): 0.43,
    ("act", "raw"): 0.92, ("act", "square"): 0.92, ("act", "exp"): 0.47, ("act", "gelu"): 2.2, ("act", "x_t"): 0.48,
    ("act", "ln"): 0.6, ("act", "guess"): 0.6,
    ("dve", "stat"): 0.2, ("dve", "norm"): 0.26, ("dve", "x_t"): 0.6, ("dve", "cos"): 0.58, ("dve", "ss"): 0.65,
    ("dve", "turned"): 1.15, ("dve", "scaled"): 1.15, ("dve", "k_t"): 0.6, ("dve", "max"): 0.3, ("dve", "inv"): 0.1,
    ("dve", "prob_t"): 0.45, ("dve", "gate"): 0.6, ("dve", "hidden"): 0.65, ("dve", "resid"): 1.15,
    ("pool", "sin"): 1.25, ("pool", "rn"): 2.6, ("pool", "rstd"): 0.7, ("pool", "weight"): 0.4, ("pool", "bias"): 2.0,
    ("pool", "close"): 1.6,
    ("sp", "shift"): 2.5, ("sp", "spread"): 2.5, ("sp", "back"): 2.5,
}
PLAN = [("a", 0), ("f", 0), ("f", 1), ("b", 0), ("f", 0), ("f", 1)]


def constants():
    half = np.arange(0, HD, 2, dtype=np.float32)
    inv_freq = (1.0 / np.float32(10000.0) ** (half / np.float32(HD))).astype(np.float32)
    t = np.arange(TOKENS, dtype=np.float32)
    freqs = (t[:, None] * inv_freq[None, :]).astype(np.float32)
    freqs = np.concatenate([freqs, freqs], axis=-1)
    base = (half + 0.4 * HD) / (1.4 * HD)
    power = (t - TOKENS // 2) / float(WINDOW // 2)
    scale = base[None, :].astype(np.float64) ** power[:, None].astype(np.float64)
    scale = np.concatenate([scale, scale], axis=-1)
    cos, sin = np.cos(freqs.astype(np.float64)), np.sin(freqs.astype(np.float64))
    sign = np.where(np.arange(HD) < HD // 2, -1.0, 1.0)
    tables = [8.0 * cos * scale, 8.0 * sin * sign * scale, cos / scale, sin * sign / scale]
    rotary = np.stack([x.reshape(TILES, P, HD) for x in tables]).transpose(2, 0, 1, 3)
    i, j = np.arange(P)[:, None], np.arange(P)[None, :]
    own = np.where(j > i, MASKED, 0.0)
    previous = np.where(j < i, MASKED, 0.0)
    return {
        "ident": np.eye(P), "rotary": rotary,
        "local_mask": np.concatenate([previous, own], axis=1),
        "causal_mask": own,
        "dot_rows": (np.arange(P)[:, None] % BROW < BHD) * 1.0,
    }


WINDOW = 128


def kernel(**inputs):
    import concourse.bacc as bacc
    from concourse.bass_utils import run_bass_kernel_spmd

    given = {k: np.asarray(v) for k, v in inputs.items()}
    a, bb, f = "L0_attn_a_", "L0_attn_b_", "L0_ffn_"
    arrays = {
        "x": given[a + "x"], "a_wq_t": given[a + "Wq"].T, "a_wd_t": given[a + "Wkv_down"].T,
        "a_wk_t": given[a + "Wk_up"].T, "a_wv_t": given[a + "Wv_up"].T, "a_wo_t": given[a + "Wo"].T,
        "b_wqkv": given[bb + "w_qkv"], "b_bqkv": given[bb + "b_qkv"], "b_wout": given[bb + "w_out"],
        "b_bout": given[bb + "b_out"], "f_wqkv": given[f + "wqkv"], "f_qs": given[f + "q_scale"],
        "f_ks": given[f + "k_scale"], "f_wo": given[f + "wo"], "f_lg": given[f + "ln_g"], "f_lb": given[f + "ln_b"],
        "f_w1": given[f + "w1"], "f_b1": given[f + "b1"], "f_w2": given[f + "w2"], "f_b2": given[f + "b2"],
    }
    arrays.update({k: v.astype(np.float32) for k, v in constants().items()})
    arrays = {"in_" + k: np.ascontiguousarray(v) for k, v in arrays.items()}
    nc = bacc.Bacc("TRN2", target_bir_lowering=False, num_devices=1)
    d = {k[3:]: nc.dram_tensor(k, v.shape, F32, kind="ExternalInput").ap() for k, v in arrays.items()}
    d["out"] = nc.dram_tensor("out", (SEQS, TOKENS, DIM), F32, kind="ExternalOutput").ap()
    d["saved"] = nc.dram_tensor("saved", (SEQS, P, TILES * DIM), F32).ap()
    build(nc, d)
    result = run_bass_kernel_spmd(nc, [arrays], core_ids=[0])
    return result.results[0]["out"]
```
